# Optimizing a Trainium2 kernel written in Bass

```python
import numpy as np
import jax
import jax.numpy as jnp

def _softmax(x, axis=-1):
    return jax.nn.softmax(x, axis=axis)

def _gelu(x):
    return jax.nn.gelu(x, approximate=True)

def _silu(x):
    return jax.nn.silu(x)

def _sigmoid(x):
    return jax.nn.sigmoid(x)

def _layernorm(x, axis=-1, eps=1e-05):
    m = jnp.mean(x, axis=axis, keepdims=True)
    v = jnp.var(x, axis=axis, keepdims=True)
    return (x - m) / jnp.sqrt(v + eps)

def _scatter_add(tgt, idx, src, axis=0):
    return tgt.at[idx].add(src)

def _segment_sum(src, seg, n):
    return jax.ops.segment_sum(src, seg, n)
kernel_name = 'mk_adaln_d1_jaxref_r8_ff96c9'

def setup_inputs(seed: int=0):
    np.random.seed(seed)
    _w = jnp.asarray

    def _L0_attn_setup():
        import jax, jax.numpy as jnp
        import numpy as np
        B, S, E, H = (2, 256, 128, 16)
        HD = E // H

        def _rope_tables(seq_len, head_dim, dtype=jnp.float32):
            i = jnp.arange(head_dim // 2, dtype=dtype)
            angles = jnp.power(jnp.asarray(10000.0, dtype), 2.0 * i / head_dim)
            theta = jnp.arange(seq_len, dtype=dtype)[:, None] * angles[None, :]
            cos = jnp.cos(theta)[None, :, None, :]
            sin = jnp.sin(theta)[None, :, None, :]
            return (cos, sin)

        def _apply_rope(t, cos, sin):
            tr, ti = (t[..., 0::2], t[..., 1::2])
            out_r = tr * cos - ti * sin
            out_i = tr * sin + ti * cos
            return jnp.stack([out_r, out_i], axis=-1).reshape(t.shape)
        key = jax.random.key(seed)
        ks = jax.random.split(key, 5)
        x = jax.random.normal(ks[0], (B, S, E), dtype=jnp.float32)
        w_q = jax.random.normal(ks[1], (H * HD, E), dtype=jnp.float32) * 0.02
        w_k = jax.random.normal(ks[2], (H * HD, E), dtype=jnp.float32) * 0.02
        w_v = jax.random.normal(ks[3], (H * HD, E), dtype=jnp.float32) * 0.02
        w_o = jax.random.normal(ks[4], (E, H * HD), dtype=jnp.float32) * 0.02
        return {'x': x, 'w_q': w_q, 'w_k': w_k, 'w_v': w_v, 'w_o': w_o}
    _L0_attn_in = _L0_attn_setup()

    def _L0_ffn_setup():
        import jax, jax.numpy as jnp
        import numpy as np
        import math
        D_IN = 128
        FEATURES = (512, 512, 128)
        BATCH, SEQ = (8, 256)

        def _conn_dense(kernel_bool, x):
            w = jnp.where(kernel_bool, jnp.float32(1.0), jnp.float32(-1.0))
            return x @ w
        key = jax.random.key(seed)
        kx, kk0, kk1, kk2 = jax.random.split(key, 4)
        x = jax.random.normal(kx, (BATCH, SEQ, D_IN), dtype=jnp.float32)
        k0 = jax.random.randint(kk0, (2 * D_IN, FEATURES[0]), 0, 2).astype(jnp.bool_)
        k1 = jax.random.randint(kk1, (FEATURES[0], FEATURES[1]), 0, 2).astype(jnp.bool_)
        k2 = jax.random.randint(kk2, (FEATURES[1], FEATURES[2]), 0, 2).astype(jnp.bool_)
        s0 = jnp.asarray(1.0 / math.sqrt(2 * D_IN), dtype=jnp.float32)
        s1 = jnp.asarray(1.0 / math.sqrt(FEATURES[0]), dtype=jnp.float32)
        s2 = jnp.asarray(1.0 / math.sqrt(FEATURES[1]), dtype=jnp.float32)
        return {'x': x, 'k0': k0, 'k1': k1, 'k2': k2, 's0': s0, 's1': s1, 's2': s2}
    _L0_ffn_in = _L0_ffn_setup()
    _L0_c = _w((lambda *s: np.random.randn(*s).astype(np.float32) * 0.05)(16, 128))
    _L0_wmod = _w((lambda *s: np.random.randn(*s).astype(np.float32) * 0.05)(128, 6 * 128) * 128 ** (-0.5))
    _d = {'L0_attn_x': _L0_attn_in['x'], 'L0_attn_w_q': _L0_attn_in['w_q'], 'L0_attn_w_k': _L0_attn_in['w_k'], 'L0_attn_w_v': _L0_attn_in['w_v'], 'L0_attn_w_o': _L0_attn_in['w_o'], 'L0_ffn_k0': _L0_ffn_in['k0'], 'L0_ffn_k1': _L0_ffn_in['k1'], 'L0_ffn_k2': _L0_ffn_in['k2'], 'L0_ffn_s0': _L0_ffn_in['s0'], 'L0_ffn_s1': _L0_ffn_in['s1'], 'L0_ffn_s2': _L0_ffn_in['s2'], 'L0_c': _L0_c, 'L0_wmod': _L0_wmod}
    _x0 = _d['L0_attn_x']
    _d['L0_attn_x'] = jax.random.normal(jax.random.fold_in(jax.random.key(seed), 1), (16, 256, 128), dtype=_x0.dtype)
    del _x0
    return _d

def reference(L0_attn_x, L0_attn_w_q, L0_attn_w_k, L0_attn_w_v, L0_attn_w_o, L0_ffn_k0, L0_ffn_k1, L0_ffn_k2, L0_ffn_s0, L0_ffn_s1, L0_ffn_s2, L0_c, L0_wmod):

    def _L0_attn_ref(x, w_q, w_k, w_v, w_o):
        import jax, jax.numpy as jnp
        import numpy as np
        B, S, E, H = (2, 256, 128, 16)
        HD = E // H

        def _rope_tables(seq_len, head_dim, dtype=jnp.float32):
            i = jnp.arange(head_dim // 2, dtype=dtype)
            angles = jnp.power(jnp.asarray(10000.0, dtype), 2.0 * i / head_dim)
            theta = jnp.arange(seq_len, dtype=dtype)[:, None] * angles[None, :]
            cos = jnp.cos(theta)[None, :, None, :]
            sin = jnp.sin(theta)[None, :, None, :]
            return (cos, sin)

        def _apply_rope(t, cos, sin):
            tr, ti = (t[..., 0::2], t[..., 1::2])
            out_r = tr * cos - ti * sin
            out_i = tr * sin + ti * cos
            return jnp.stack([out_r, out_i], axis=-1).reshape(t.shape)
        b, s, _ = x.shape
        q = (x @ w_q.T).reshape(b, s, H, HD)
        k = (x @ w_k.T).reshape(b, s, H, HD)
        v = (x @ w_v.T).reshape(b, s, H, HD)
        cos, sin = _rope_tables(s, HD, x.dtype)
        q = _apply_rope(q, cos, sin)
        k = _apply_rope(k, cos, sin)
        att = jnp.einsum('bqhd,bkhd->bhqk', q, k) / jnp.sqrt(jnp.asarray(HD, x.dtype))
        att = jax.nn.softmax(att, axis=-1)
        y = jnp.einsum('bhqk,bkhd->bqhd', att, v).reshape(b, s, H * HD)
        return y @ w_o.T

    def _L0_ffn_ref(x, k0, k1, k2, s0, s1, s2):
        import jax, jax.numpy as jnp
        import numpy as np
        import math
        D_IN = 128
        FEATURES = (512, 512, 128)
        BATCH, SEQ = (8, 256)

        def _conn_dense(kernel_bool, x):
            w = jnp.where(kernel_bool, jnp.float32(1.0), jnp.float32(-1.0))
            return x @ w
        h = jnp.concatenate([x, -x], axis=-1)
        h = s0 * _conn_dense(k0, h)
        h = jax.nn.relu(h) * 2
        h = s1 * _conn_dense(k1, h)
        h = jax.nn.relu(h) * 2
        h = s2 * _conn_dense(k2, h)
        return h
    x = L0_attn_x
    mod = (_silu(L0_c) @ L0_wmod).reshape(L0_c.shape[0], 6, 1, -1)
    sa, ca, ga, sb, cb, gb = (mod[:, 0], mod[:, 1], mod[:, 2], mod[:, 3], mod[:, 4], mod[:, 5])
    ga = (2 * (ga >= 0) - 1) * jnp.maximum(jnp.abs(ga), 0.25)
    gb = (2 * (gb >= 0) - 1) * jnp.maximum(jnp.abs(gb), 0.25)
    h = _layernorm(x, axis=-1) * (1 + ca) + sa
    x = x + ga * _L0_attn_ref(h, L0_attn_w_q, L0_attn_w_k, L0_attn_w_v, L0_attn_w_o)
    h = _layernorm(x, axis=-1) * (1 + cb) + sb
    x = x + gb * _L0_ffn_ref(h, L0_ffn_k0, L0_ffn_k1, L0_ffn_k2, L0_ffn_s0, L0_ffn_s1, L0_ffn_s2)
    return x

_drawn_inputs = setup_inputs


def setup_inputs(seed=0):
    import zlib

    import numpy as np

    out = dict(_drawn_inputs(seed))
    spreads = {}
    factors = {'L0_attn_w_q': 8.0, 'L0_attn_w_k': 8.0, 'L0_attn_w_v': 8.0, 'L0_attn_w_o': 8.0}
    for name, (base, spread) in spreads.items():
        noise = np.random.default_rng([zlib.crc32(name.encode()), seed]).standard_normal(out[name].shape)
        drawn = base * np.exp(spread * noise) if base else spread * noise
        out[name] = jnp.asarray(drawn.astype(out[name].dtype))
    for name, factor in factors.items():
        out[name] = (out[name] * factor).astype(out[name].dtype)
    return out
```

```python
import concourse.bass as bass
from concourse import mybir
from contextlib import ExitStack
import numpy as np

BATCHES, SEQ, EMB, HEADS = 16, 256, 128, 16
HEAD_DIM = EMB // HEADS
HIDDEN = 512
LANES = 128
TILES = SEQ // LANES
PARTS = 3
PRODUCTS = [(0, 0), (0, 1), (0, 2), (1, 0), (1, 1), (2, 0)]
STACK = len(PRODUCTS) * HEAD_DIM
SCORE_ROWS = STACK + PARTS
MCOLS = PARTS * HEADS
RING = 4
QUAD = 4
EPS = 1e-5
GROUP = 4
GROUPS = BATCHES * TILES // GROUP
BLOCKS = HIDDEN // LANES
LEAD = HEADS // 2


class Batch:

    def __init__(self, turn, k):
        self.turn, self.k = turn, k
        self.slot, self.pair = k % RING, k % 2
        self.known = k if isinstance(turn, int) else None

    def plus(self, d):
        return Batch(self.turn, self.k + d)

    def exists(self):
        return self.known is None or 0 <= self.known < BATCHES

    def number(self):
        return self.turn * RING + self.k

    def count(self, each, extra):
        return self.turn * (RING * each) + (self.k * each + extra)

    def in_slot(self, each):
        return self.turn * each + (self.k // RING + 1) * each

    def capped(self, ahead):
        n = self.count(1, ahead)
        return min(n, BATCHES) if isinstance(n, int) else n


def wait(engine, sem, value):
    if not isinstance(value, int) or value > 0:
        engine.wait_ge(sem, value)


def adaln_block(nc: bass.Bass, x, wq, wk, wv, wo, rope, eye, c_t, wmod, k0, k1, k2, scales, out):
    f32, f32r, bf16, u8 = mybir.dt.float32, mybir.dt.float32r, mybir.dt.bfloat16, mybir.dt.uint8
    ALU, ACT, AX = mybir.AluOpType, mybir.ActivationFunctionType, mybir.AxisListType
    x_v = x.rearrange("b (p t) e -> p b t e", t=TILES)
    out_v = out.rearrange("b (p t) e -> p b t e", t=TILES)

    ctx = ExitStack()
    with ctx:
        def sb(name, shape, dt=f32):
            return ctx.enter_context(nc.sbuf_tensor(name, shape, dt))

        def ps(name, shape):
            return ctx.enter_context(nc.psum_tensor(name, shape, f32))

        def sem(name):
            return ctx.enter_context(nc.semaphore(name))

        X = sb("X", [LANES, BATCHES, TILES, EMB])
        WQ = sb("WQ", [EMB, 2, EMB])
        WK = sb("WK", [EMB, 2, EMB])
        WV = sb("WV", [EMB, EMB])
        WO = sb("WO", [EMB, EMB])
        ROPE = sb("ROPE", [LANES, 2, 2 * SEQ])
        EYE = sb("EYE", [LANES, LANES])
        EYEB = sb("EYEB", [LANES, LANES], bf16)
        CT = sb("CT", [EMB, BATCHES])
        SILU = sb("SILU", [EMB, 3, BATCHES])
        WMOD = sb("WMOD", [EMB, 6 * EMB])
        MOD = sb("MOD", [EMB, 6, BATCHES])
        GATE = sb("GATE", [EMB, 4, 2, BATCHES])
        SCALE = sb("SCALE", [LANES, 3])
        BN = sb("BN", [LANES, TILES, 6])
        MEANVAR = sb("MEANVAR", [LANES, 2, TILES, 2])
        CONST = sb("CONST", [LANES, 3, GROUP])
        LN = sb("LN", [LANES, 4, TILES])
        XH = sb("XH", [LANES, TILES, EMB])
        HT = sb("HT", [EMB, SEQ])
        TURNED = sb("TURNED", [LANES, 2, 2 * SEQ])
        QK = sb("QK", [LANES, 2, SEQ])
        REST = sb("REST", [LANES, 2, SEQ])
        QKP = sb("QKP", [LANES, 2, PARTS, SEQ], bf16)
        ST = [sb(f"ST{r}", [LANES, HEADS // 2, 2, SEQ], bf16) for r in range(RING)]
        VS = [sb(f"VS{r}", [LANES, TILES, HEADS, 32]) for r in range(RING)]
        NMAX = sb("NMAX", [LANES, 2, TILES, 2, HEADS // 2])
        NREST = sb("NREST", [LANES, TILES, 2, HEADS // 2])
        NPART = sb("NPART", [LANES, TILES, LANES], bf16)
        MROW = sb("MROW", [MCOLS, SEQ], bf16)
        PT = sb("PT", [LANES, 2 * QUAD, TILES, SEQ])
        OTS = sb("OTS", [LANES, HEADS // QUAD, SEQ])
        RDEN = sb("RDEN", [LANES, TILES, HEADS])
        YN = sb("YN", [LANES, TILES, EMB])
        YT = sb("YT", [EMB, SEQ])
        OE = sb("OE", [EMB, SEQ])
        U0 = sb("U0", [EMB, 2, HIDDEN], u8)
        U1 = sb("U1", [LANES, BLOCKS, HIDDEN], u8)
        U2 = sb("U2", [LANES, BLOCKS, EMB], u8)
        W0 = sb("W0", [EMB, HIDDEN], f32r)
        W1 = sb("W1", [LANES, BLOCKS, HIDDEN], f32r)
        W2 = sb("W2", [LANES, BLOCKS, EMB], f32r)
        FBN = sb("FBN", [LANES, GROUP, 6])
        FMV = sb("FMV", [LANES, GROUP, 2])
        FLN = sb("FLN", [LANES, 4, GROUP])
        FXH = sb("FXH", [LANES, GROUP, EMB])
        FH = sb("FH", [EMB, 2, SEQ])
        FHHI = sb("FHHI", [EMB, 2 * SEQ], f32r)
        FHLO = sb("FHLO", [EMB, 2 * SEQ], f32r)
        RAW = sb("RAW", [LANES, BLOCKS, GROUP * LANES])
        HI = [sb(f"HI{n}", [LANES, BLOCKS, GROUP * LANES], f32r) for n in range(2)]
        LO = [sb(f"LO{n}", [LANES, BLOCKS, GROUP * LANES], f32r) for n in range(2)]
        FY = sb("FY", [EMB, 2, SEQ])
        OUT = sb("OUT", [LANES, GROUP, EMB])

        S1 = [ps(f"S1{n}", [LANES, TILES, SEQ]) for n in range(3)]
        S2 = [ps(f"S2{n}", [LANES, TILES, SEQ]) for n in range(2)]
        OT = ps("OT", [LANES, 2, SEQ])
        PA = ps("PA", [LANES, 2 * SEQ])
        PB = ps("PB", [LANES, 2 * SEQ])

        x_loaded = [sem(f"x_loaded{n}") for n in range(4)]
        w_loaded = sem("w_loaded")
        mod_loaded = sem("mod_loaded")
        ffn_loaded = sem("ffn_loaded")
        ones_set, eyeb_set = sem("ones_set"), sem("eyeb_set")
        c_exp, silu_step, mod_ready, mod_step = sem("c_exp"), sem("silu_step"), sem("mod_ready"), sem("mod_step")
        bn_ready, stats_ready, ln_step, ln_ready = sem("bn_ready"), sem("stats_ready"), sem("ln_step"), sem("ln_ready")
        xhat_ready, xT_ready, hT_ready = sem("xhat_ready"), sem("xT_ready"), sem("hT_ready")
        q_ready, k_ready, v_ready, v_copied = sem("q_ready"), sem("k_ready"), sem("v_ready"), sem("v_copied")
        turned_q, turned_k, sum_ready = sem("turned_q"), sem("turned_k"), sem("sum_ready")
        part1, rest_ready, part2, part3 = sem("part1"), sem("rest_ready"), sem("part2"), sem("part3")
        stack_ready = [sem(f"stack_ready{n}") for n in range(RING)]
        mrows_ready = [sem(f"mrows_ready{n}") for n in range(RING)]
        s1_ready, max_ready, mpart_step, mparts_ready = sem("s1_ready"), sem("max_ready"), sem("mpart_step"), sem("mparts_ready")
        mT_ready, mT_copied = sem("mT_ready"), sem("mT_copied")
        s2_ready, exp_ready, pv_ready, ot_copied = sem("s2_ready"), sem("exp_ready"), sem("pv_ready"), sem("ot_copied")
        y_turned, rden_ready, y_normed = sem("y_turned"), sem("rden_ready"), sem("y_normed")
        yT_ready, yT_copied, o_ready, o_gated = sem("yT_ready"), sem("yT_copied"), sem("o_ready"), sem("o_gated")
        o_turned, x1_ready = sem("o_turned"), sem("x1_ready")
        fw_ready = sem("fw_ready")
        f_bn, f_stats, f_ln_step, f_ln = sem("f_bn"), sem("f_stats"), sem("f_ln_step"), sem("f_ln")
        f_xhat, f_xT, f_hT, f_hhi, f_hlo = sem("f_xhat"), sem("f_xT"), sem("f_hT"), sem("f_hhi"), sem("f_hlo")
        block_ready, raw_ready, hi_ready = sem("block_ready"), sem("raw_ready"), sem("hi_ready")
        lo_even, lo_odd = sem("lo_even"), sem("lo_odd")
        y_ready, y_gated, y_back, out_ready, out_stored = (sem("y_ready"), sem("y_gated"), sem("y_back"),
                                                           sem("out_ready"), sem("out_stored"))

        STACK_DMAS = 2 * len(PRODUCTS)
        X_CHUNKS = [0, 1, 4, 8, 16]

        def s1_bank(h):
            return 1 if h == HEADS - 1 else h % 3

        def s1_bank_read(h):
            before = [g for g in range(h - HEADS, h) if s1_bank(g % HEADS) == s1_bank(h)]
            return before[-1] + 1

        def x_chunk(b):
            return max(n for n in range(4) if X_CHUNKS[n] <= b)

        block = ctx.enter_context(nc.Block())

        @block.sync
        def _(sp):
            for n in range(4):
                sp.dma_start(X[:, X_CHUNKS[n]:X_CHUNKS[n + 1]], x_v[:, X_CHUNKS[n]:X_CHUNKS[n + 1]]).then_inc(x_loaded[n], 16)
                if n == 0:
                    sp.dma_start(CT[:, :], c_t).then_inc(mod_loaded, 16)
                    sp.dma_start(WMOD[:, :], wmod).then_inc(mod_loaded, 16)
                    sp.dma_start(SCALE[:, :], scales.to_broadcast([LANES, 3])).then_inc(mod_loaded, 16)
                    sp.dma_start(EYE[:, :], eye).then_inc(w_loaded, 16)
                    for dst, src in ((WQ, wq), (WK, wk), (ROPE, rope)):
                        sp.dma_start(dst[:, :, :], src).then_inc(w_loaded, 16)
                    for dst, src in ((WV, wv), (WO, wo)):
                        sp.dma_start(dst[:, :], src).then_inc(w_loaded, 16)
            sp.dma_start(U0[:, :, :], k0.rearrange("(s p) n -> p s n", s=2)).then_inc(ffn_loaded, 16)
            sp.dma_start(U1[:, :, :], k1.rearrange("(s p) n -> p s n", s=BLOCKS)).then_inc(ffn_loaded, 16)
            sp.dma_start(U2[:, :, :], k2.rearrange("(s p) n -> p s n", s=BLOCKS)).then_inc(ffn_loaded, 16)

            def stack(b, parts, last):
                wait(sp, parts, b.count(1, 1))
                if b.known is not None and b.known < RING and last == 0:
                    sp.wait_ge(ones_set, b.known + 1)
                for j, (qp, kp) in enumerate(PRODUCTS):
                    for half in range(2 if max(qp, kp) == last else 0):
                        row, src = 64 * half + HEAD_DIM * j, QKP[64 * half:64 * half + 64, :, :, :]
                        src = src.rearrange("p a c t -> p (a c) t")[:, qp:PARTS + kp + 1:PARTS + kp - qp, :]
                        sp.dma_start(ST[b.slot][row:row + HEAD_DIM, :, :, :], src).then_inc(stack_ready[b.slot], 16)

            def max_rows(b):
                wait(sp, mT_copied, b.count(1, 1))
                for half in range(2):
                    row, n = 64 * half + STACK, PARTS * HEADS // 2
                    sp.dma_start(ST[b.slot][row:row + PARTS, :, 0, :],
                                 MROW[half * n:(half + 1) * n, :]).then_inc(mrows_ready[b.slot], 16)

            def whole_stack(b):
                for last, parts in enumerate((part1, part2, part3)):
                    stack(b, parts, last)

            def iteration(b):
                if b.plus(1).exists():
                    max_rows(b.plus(1))
                if b.plus(3).exists():
                    whole_stack(b.plus(3))

            whole_stack(Batch(0, 0))
            whole_stack(Batch(0, 1))
            max_rows(Batch(0, 0))
            whole_stack(Batch(0, 2))
            iteration(Batch(0, 0))
            with sp.Fori(0, 3) as turn:
                for j in range(RING):
                    iteration(Batch(turn, 1 + j))
            for b in range(13, BATCHES):
                iteration(Batch(0, b))

            for g in range(GROUPS):
                sp.wait_ge(out_ready, g + 1)
                sp.dma_start(out_v[:, 2 * g:2 * g + 2, :, :], OUT[:, :, :]).then_inc(out_stored, 16)
            sp.wait_ge(out_stored, 16 * GROUPS)

        @block.gpsimd
        def _(pool):
            for n, value in enumerate((-0.5, EPS, -1.0)):
                pool.memset(CONST[:, n, :], value)
            pool.memset(NPART[:, :, :], 0.0)
            def constants(r):
                pool.memset(ST[r][:, :, 1, :], 1.0)
                pool.memset(VS[r][:, :, :, HEAD_DIM + 1:32], 0.0)
                pool.memset(VS[r][:, :, :, HEAD_DIM:HEAD_DIM + 1], 1.0).then_inc(ones_set, 1)

            def layer_norm(b):
                wait(pool, stats_ready, b.count(1, 1))
                wait(pool, xhat_ready, b.count(1, 0))
                mv = MEANVAR[:, b.pair]
                pool.tensor_tensor(LN[:, 0, :], mv[:, :, 1], CONST[:, 1, 0:TILES], ALU.add).then_inc(ln_step, 1)
                wait(pool, ln_step, b.count(3, 1))
                pool.tensor_tensor(LN[:, 1, :], LN[:, 0, :], CONST[:, 0, 0:TILES], ALU.pow).then_inc(ln_step, 1)
                wait(pool, ln_step, b.count(3, 2))
                pool.tensor_tensor(LN[:, 2, :], mv[:, :, 0], LN[:, 1, :], ALU.mult).then_inc(ln_step, 1)
                wait(pool, ln_step, b.count(3, 3))
                pool.tensor_tensor(LN[:, 3, :], LN[:, 2, :], CONST[:, 2, 0:TILES], ALU.mult).then_inc(ln_ready, 1)

            def rotate_and_split(b):
                wait(pool, turned_k, b.count(1, 1))
                wait(pool, part3, b.count(1, 0))
                pool.tensor_tensor(QK[:, :, :], TURNED[:, :, 0:SEQ], TURNED[:, :, SEQ:2 * SEQ],
                                   ALU.add).then_inc(sum_ready, 1)
                if b.k > 0 or b.known is None:
                    before = b.plus(-1)
                    wait(pool, stack_ready[before.slot], before.in_slot(16 * STACK_DMAS))
                wait(pool, s2_ready, b.count(HEADS, -(RING - 1) * HEADS))
                pool.tensor_tensor(QKP[:, :, 0, :], TURNED[:, :, 0:SEQ], TURNED[:, :, SEQ:2 * SEQ],
                                   ALU.add).then_inc(part1, 1)
                wait(pool, sum_ready, b.count(1, 1))
                wait(pool, part1, b.count(1, 1))
                pool.tensor_tensor(QKP[:, :, 1, :], QK[:, :, :], QKP[:, :, 0, :], ALU.subtract).then_inc(part2, 1)
                pool.tensor_tensor(REST[:, :, :], QK[:, :, :], QKP[:, :, 0, :], ALU.subtract).then_inc(rest_ready, 1)
                wait(pool, rest_ready, b.count(1, 1))
                wait(pool, part2, b.count(1, 1))
                pool.tensor_tensor(QKP[:, :, 2, :], REST[:, :, :], QKP[:, :, 1, :], ALU.subtract).then_inc(part3, 1)

            def iteration(b):
                if b.plus(3).exists():
                    layer_norm(b.plus(3))
                    rotate_and_split(b.plus(3))

            constants(0)
            pool.wait_ge(ones_set, 1)
            for n in range(3):
                layer_norm(Batch(0, n))
                constants(n + 1)
                rotate_and_split(Batch(0, n))
            iteration(Batch(0, 0))
            with pool.Fori(0, 3) as turn:
                for j in range(RING):
                    iteration(Batch(turn, 1 + j))

            pool.wait_ge(ffn_loaded, 48)
            pool.tensor_scalar(W1[:, :, :], U1[:, :, :], 2.0, -1.0, ALU.mult, ALU.add).then_inc(fw_ready, 1)
            pool.tensor_scalar(W2[:, :, :], U2[:, :, :], 2.0, -1.0, ALU.mult, ALU.add).then_inc(fw_ready, 1)

            def f_norm(g):
                pool.wait_ge(f_stats, g + 1)
                if not isinstance(g, int) or g > 0:
                    pool.wait_ge(f_xhat, g)
                pool.tensor_tensor(FLN[:, 0, :], FMV[:, :, 1], CONST[:, 1, :], ALU.add).then_inc(f_ln_step, 1)
                pool.wait_ge(f_ln_step, g * 3 + 1)
                pool.tensor_tensor(FLN[:, 1, :], FLN[:, 0, :], CONST[:, 0, :], ALU.pow).then_inc(f_ln_step, 1)
                pool.wait_ge(f_ln_step, g * 3 + 2)
                pool.tensor_tensor(FLN[:, 2, :], FMV[:, :, 0], FLN[:, 1, :], ALU.mult).then_inc(f_ln_step, 1)
                pool.wait_ge(f_ln_step, g * 3 + 3)
                pool.tensor_tensor(FLN[:, 3, :], FLN[:, 2, :], CONST[:, 2, :], ALU.mult).then_inc(f_ln, 1)

            def h_low(g):
                pool.wait_ge(f_hhi, g + 1)
                pool.tensor_tensor(FHLO[:, :], FH[:, :, :].rearrange("p a t -> p (a t)"),
                                   FHHI[:, :].bitcast(f32), ALU.subtract).then_inc(f_hlo, 1)

            def low(g, layer, kb):
                pool.wait_ge(hi_ready, g * 8 + (4 * layer + kb + 1))
                pool.tensor_tensor(LO[layer][:, kb, :], RAW[:, kb, :], HI[layer][:, kb, :].bitcast(f32),
                                   ALU.subtract).then_inc(lo_even, 1)

            def f_first():
                f_norm(0)
                h_low(0)
                low(0, 0, 0)
                low(0, 0, 2)

            def f_group(g, more):
                if more:
                    f_norm(g + 1)
                low(g, 1, 0)
                if more:
                    h_low(g + 1)
                low(g, 1, 2)
                if more:
                    low(g + 1, 0, 0)
                    low(g + 1, 0, 2)

            f_first()
            f_group(0, True)
            with pool.Fori(1, GROUPS - 1) as g:
                f_group(g, True)
            f_group(GROUPS - 1, False)

        @block.scalar
        def _(act):
            act.wait_ge(mod_loaded, 48)
            act.activation(SILU[:, 0, :], CT[:, :], ACT.Exp, scale=-1.0).then_inc(c_exp, 1)

            def normalise(b):
                wait(act, ln_ready, b.count(1, 1))
                wait(act, xT_ready, b.count(1, 0))
                for t in range(TILES):
                    ins = act.activation(XH[:, t, :], X[:, at(b), t, :], ACT.Identity,
                                         bias=LN[:, 3, t:t + 1], scale=LN[:, 1, t:t + 1])
                ins.then_inc(xhat_ready, 1)

            def at(b):
                return b.known if b.known is not None else bass.ds(b.number(), 1)

            def col(tile, j, b):
                n = b.number() if b.known is None else b.known
                return tile[:, j, bass.ds(n, 1)] if b.known is None else tile[:, j, n:n + 1]

            def modulate(b):
                wait(act, xT_ready, b.count(1, 1))
                if b.known == 0:
                    act.wait_ge(mod_step, 7)
                act.activation(HT[:, :], PA[:, 0:SEQ], ACT.Identity, bias=col(MOD, 0, b),
                               scale=col(MOD, 1, b)).then_inc(hT_ready, 1)

            def copy_v(b):
                wait(act, v_ready, b.count(1, 1))
                wait(act, pv_ready, b.count(4, -4 * (RING - 1)))
                if b.known is not None and b.known < RING:
                    act.wait_ge(ones_set, b.known + 1)
                act.activation(VS[b.slot][:, :, :, 0:HEAD_DIM],
                               PA[:, 0:SEQ].rearrange("p (t h d) -> p t h d", t=TILES, h=HEADS),
                               ACT.Copy).then_inc(v_copied, 1)

            def exps(b, h):
                wait(act, s2_ready, b.count(HEADS, h + 1))
                if h % QUAD == 0:
                    wait(act, pv_ready, b.count(4, h // QUAD - 1))
                act.activation(PT[:, h % (2 * QUAD), :, :], S2[h % 2][:, :, :], ACT.Exp).then_inc(exp_ready, 1)

            def copy_ot(b, half):
                wait(act, pv_ready, b.count(4, 2 * half + 2))
                wait(act, y_turned, b.count(2, 0))
                act.activation(OTS[:, 2 * half:2 * half + 2, :], OT[:, :, :],
                               ACT.Copy).then_inc(ot_copied, 1)

            def copy_yt(b):
                wait(act, yT_ready, b.count(1, 1))
                wait(act, o_ready, b.count(1, 0))
                act.activation(YT[:, :], PB[:, 0:SEQ], ACT.Copy).then_inc(yT_copied, 1)

            def copy_mt(b):
                wait(act, mT_ready, b.count(1, 1))
                if b.k > 0 or b.known is None:
                    before = b.plus(-1)
                    wait(act, mrows_ready[before.slot], before.in_slot(32))
                act.activation(MROW[:, :], MT_PSUM[0:MCOLS, :], ACT.Copy).then_inc(mT_copied, 1)

            def gate(b):
                wait(act, o_ready, b.count(1, 1))
                wait(act, o_turned, b.count(1, 0))
                act.activation(OE[:, :], PA[:, 0:SEQ], ACT.Identity, scale=col(MOD, 2, b)).then_inc(o_gated, 1)

            def iteration(b):
                tail, prep = b.plus(-1), b.plus(3)
                for h in range(HEADS):
                    if b.exists():
                        exps(b, h)
                    if tail.exists():
                        if h == 1:
                            copy_ot(tail, 1)
                        if h == 11:
                            copy_yt(tail)
                        if h == 13:
                            gate(tail)
                    if b.plus(2).exists() and h == 2:
                        copy_v(b.plus(2))
                    if prep.exists():
                        if h == 3:
                            normalise(prep)
                        if h == 5:
                            modulate(prep)
                    if b.exists() and h == 9:
                        copy_ot(b, 0)
                    if b.plus(1).exists() and h == 9:
                        copy_mt(b.plus(1))

            MT_PSUM = PB[:, 0:SEQ // 2].bitcast(bf16)
            for n in range(3):
                normalise(Batch(0, n))
                modulate(Batch(0, n))
                if n < 2:
                    copy_v(Batch(0, n))
            copy_mt(Batch(0, 0))
            iteration(Batch(0, 0))
            with act.Fori(0, 3) as turn:
                for j in range(RING):
                    iteration(Batch(turn, 1 + j))
            for b in range(13, BATCHES + 1):
                iteration(Batch(0, b))

            def f_mod(g):
                act.wait_ge(f_xT, g + 1)
                if not isinstance(g, int) or g > 0:
                    act.wait_ge(f_hlo, g)
                for u in range(2):
                    n = g * 2 + u
                    c = slice(n, n + 1) if isinstance(g, int) else bass.ds(n, 1)
                    ins = act.activation(FH[:, u, :], PA[:, u * SEQ:(u + 1) * SEQ], ACT.Identity,
                                         bias=MOD[:, 3, c], scale=MOD[:, 4, c])
                ins.then_inc(f_hT, 1)

            def f_relu(g, layer, kb):
                act.wait_ge(block_ready, g * 8 + (4 * layer + kb + 1))
                if not isinstance(g, int) or g > 0 or layer > 0:
                    act.wait_ge(hi_ready, g * 8 + (4 * layer + kb - 3))
                    act.wait_ge(lo_odd if kb % 2 else lo_even, g * 4 + (2 * layer + kb // 2 - 1))
                bank = (S1 + S2)[kb]
                act.activation(RAW[:, kb, :], bank[:, :, :].rearrange("p a t -> p (a t)"), ACT.Relu,
                               scale=SCALE[:, layer:layer + 1]).then_inc(raw_ready, 1)

            def f_gate(g):
                act.wait_ge(y_ready, g + 1)
                if not isinstance(g, int) or g > 0:
                    act.wait_ge(y_back, g)
                for u in range(2):
                    n = g * 2 + u
                    c = slice(n, n + 1) if isinstance(g, int) else bass.ds(n, 1)
                    ins = act.activation(FY[:, u, :], PB[:, u * SEQ:(u + 1) * SEQ], ACT.Identity,
                                         scale=MOD[:, 5, c])
                ins.then_inc(y_gated, 1)

            def f_group(g, more):
                f_relu(g, 1, 0)
                f_relu(g, 1, 1)
                if more:
                    f_mod(g + 1)
                f_relu(g, 1, 2)
                f_relu(g, 1, 3)
                if more:
                    for kb in range(BLOCKS):
                        f_relu(g + 1, 0, kb)
                f_gate(g)

            f_mod(0)
            for kb in range(BLOCKS):
                f_relu(0, 0, kb)
            f_group(0, True)
            with act.Fori(1, GROUPS - 1) as g:
                f_group(g, True)
            f_group(GROUPS - 1, False)

        @block.vector
        def _(dve):
            dve.wait_ge(c_exp, 1)
            dve.tensor_scalar(SILU[:, 1, :], SILU[:, 0, :], 1.0, None, ALU.add).then_inc(silu_step, 1)
            dve.wait_ge(silu_step, 1)
            dve.reciprocal(SILU[:, 2, :], SILU[:, 1, :]).then_inc(silu_step, 1)
            dve.wait_ge(silu_step, 2)
            dve.tensor_tensor(SILU[:, 0, :], SILU[:, 2, :], CT[:, :], ALU.mult).then_inc(silu_step, 1)
            dve.wait_ge(w_loaded, 96)
            dve.tensor_copy(EYEB[:, :], EYE[:, :]).then_inc(eyeb_set, 1)

            def at(b):
                return b.known if b.known is not None else bass.ds(b.number(), 1)

            def statistics(b):
                if b.known is not None and b.known < 4:
                    dve.wait_ge(x_loaded[x_chunk(b.known)], 16)
                wait(dve, stats_ready, b.count(1, 0))
                wait(dve, ln_ready, b.count(1, -1))
                for t in range(TILES):
                    dve.bn_stats(BN[:, t, :], X[:, at(b), t, :]).then_inc(bn_ready, 1)

            def aggregate(b):
                for t in range(TILES):
                    ins = dve.bn_aggr(MEANVAR[:, b.pair, t, :], BN[:, t, :])
                ins.then_inc(stats_ready, 1)

            def modulation():
                dve.wait_ge(mod_ready, 1)
                dve.tensor_copy(MOD[:, :, :], PB[:, 0:6 * BATCHES].rearrange("p (j b) -> p j b", j=6)).then_inc(mod_step, 1)
                dve.wait_ge(mod_step, 1)
                dve.tensor_scalar(MOD[:, 1:5:3, :], MOD[:, 1:5:3, :], 1.0, None, ALU.add)
                dve.tensor_scalar(GATE[:, 0], MOD[:, 2:6:3, :], -1.0, None, ALU.mult)
                dve.tensor_scalar(GATE[:, 1], MOD[:, 2:6:3, :], 0.0, 2.0, ALU.is_ge, ALU.mult).then_inc(mod_step, 1)
                dve.wait_ge(mod_step, 2)
                dve.tensor_tensor(GATE[:, 2], MOD[:, 2:6:3, :], GATE[:, 0], ALU.max).then_inc(mod_step, 1)
                dve.wait_ge(mod_step, 3)
                dve.tensor_scalar(GATE[:, 3], GATE[:, 2], 0.25, None, ALU.max)
                dve.tensor_scalar(GATE[:, 0], GATE[:, 1], -1.0, None, ALU.add).then_inc(mod_step, 1)
                dve.wait_ge(mod_step, 4)
                dve.tensor_tensor(MOD[:, 2:6:3, :], GATE[:, 0], GATE[:, 3], ALU.mult).then_inc(mod_step, 1)
                dve.wait_ge(mod_step, 5)
                dve.tensor_scalar(MOD[:, 5, :], MOD[:, 5, :], SCALE[:, 2:3], None, ALU.mult).then_inc(mod_step, 1)
                dve.wait_ge(mod_step, 6)
                dve.tensor_scalar(SCALE[:, 0:1], SCALE[:, 0:1], 4.0, None, ALU.mult)
                dve.tensor_scalar(SCALE[:, 1:2], SCALE[:, 1:2], 2.0, None, ALU.mult).then_inc(mod_step, 1)

            def turn_q(b):
                wait(dve, q_ready, b.count(1, 1))
                wait(dve, part1, b.count(1, 0))
                dve.tensor_tensor(TURNED[:, 0, :], PA[:, :], ROPE[:, 0, :], ALU.mult).then_inc(turned_q, 1)

            def turn_k(b):
                wait(dve, k_ready, b.count(1, 1))
                dve.tensor_tensor(TURNED[:, 1, :], PA[:, :], ROPE[:, 1, :], ALU.mult).then_inc(turned_k, 1)

            def maximum(b, h):
                wait(dve, s1_ready, b.count(HEADS, h + 1))
                if h == 0:
                    wait(dve, mparts_ready, b.count(1, -1))
                dve.tensor_reduce(NMAX[:, b.pair, :, h % 2, h // 2], S1[s1_bank(h)][:, :, :], AX.X, ALU.max,
                                  negate=True).then_inc(max_ready, 1)

            def split_max(b):
                wait(dve, max_ready, b.count(HEADS, HEADS))
                wait(dve, mT_ready, b.count(1, 0))
                if b.known == 0:
                    dve.wait_ge(ones_set, 1)
                nm = NMAX[:, b.pair]
                part = NPART[:, :, 0:MCOLS].rearrange("p t (a c n) -> p t a c n", a=2, c=PARTS)
                dve.tensor_copy(part[:, :, :, 0, :], nm).then_inc(mpart_step, 1)
                wait(dve, mpart_step, b.count(3, 1))
                dve.tensor_tensor(NREST[:, :, :, :], nm, part[:, :, :, 0, :], ALU.subtract).then_inc(mpart_step, 1)
                wait(dve, mpart_step, b.count(3, 2))
                dve.tensor_copy(part[:, :, :, 1, :], NREST[:, :, :, :]).then_inc(mpart_step, 1)
                wait(dve, mpart_step, b.count(3, 3))
                dve.tensor_tensor(part[:, :, :, 2, :], NREST[:, :, :, :], part[:, :, :, 1, :],
                                  ALU.subtract).then_inc(mparts_ready, 1)

            def normalise_y(b, t):
                wait(dve, y_turned, b.count(2, t + 1))
                if t == 0:
                    wait(dve, yT_ready, b.count(1, 0))
                y = PB[:, :].rearrange("p (h c) -> p h c", c=32)
                dve.reciprocal(RDEN[:, t, :], y[:, :, HEAD_DIM]).then_inc(rden_ready, 1)
                wait(dve, rden_ready, b.count(2, t + 1))
                dve.tensor_tensor(YN[:, t, :].rearrange("p (h d) -> p h d", d=HEAD_DIM), y[:, :, 0:HEAD_DIM],
                                  RDEN[:, t, :].unsqueeze(2).to_broadcast([LANES, HEADS, HEAD_DIM]),
                                  ALU.mult).then_inc(y_normed, 1)

            def add_attention(b):
                wait(dve, o_turned, b.count(1, 1))
                xs = X[:, at(b), :, :] if b.known is not None else X[:, at(b), :, :].rearrange("p o t e -> p (o t) e")
                dve.tensor_tensor(xs, PB[:, 0:SEQ].rearrange("p (t e) -> p t e", t=TILES), xs,
                                  ALU.add).then_inc(x1_ready, 1)

            def iteration(b):
                tail, prep = b.plus(-1), b.plus(3)
                if prep.exists():
                    statistics(prep)
                for h in range(HEADS):
                    m = b.plus(1 + h // LEAD)
                    if prep.exists() and h == 0:
                        wait(dve, bn_ready, prep.count(TILES, TILES))
                    if m.exists():
                        maximum(m, (h + LEAD) % HEADS)
                    if prep.exists() and h == 0:
                        aggregate(prep)
                    if tail.exists():
                        if h == 3:
                            normalise_y(tail, 0)
                        if h == 6:
                            normalise_y(tail, 1)
                        if h == 15:
                            add_attention(tail)
                    if prep.exists():
                        if h == 7:
                            turn_q(prep)
                        if h == 10:
                            turn_k(prep)
                    if b.plus(1).exists() and h == 8:
                        split_max(b.plus(1))

            def prepare(b):
                turn_q(b)
                turn_k(b)

            MT_PSUM = PB[:, 0:SEQ // 2].bitcast(bf16)
            statistics(Batch(0, 0))
            dve.wait_ge(bn_ready, TILES * 1)
            aggregate(Batch(0, 0))
            modulation()
            statistics(Batch(0, 1))
            dve.wait_ge(bn_ready, TILES * 2)
            aggregate(Batch(0, 1))
            prepare(Batch(0, 0))
            statistics(Batch(0, 2))
            dve.wait_ge(bn_ready, TILES * 3)
            aggregate(Batch(0, 2))
            prepare(Batch(0, 1))
            for h in range(HEADS):
                maximum(Batch(0, 0), h)
            split_max(Batch(0, 0))
            prepare(Batch(0, 2))
            for h in range(LEAD):
                maximum(Batch(0, 1), h)
            for n in range(4):
                dve.wait_ge(x_loaded[n], 16)
            iteration(Batch(0, 0))
            with dve.Fori(0, 3) as turn:
                for j in range(RING):
                    iteration(Batch(turn, 1 + j))
            for b in range(13, BATCHES + 1):
                iteration(Batch(0, b))

            def tile_at(g, t, n=1):
                return slice(g * GROUP + t, g * GROUP + t + n) if isinstance(g, int) else bass.ds(g * GROUP + t, n)

            XF = X[:, :, :, :].rearrange("p b t e -> p (b t) e")

            def f_statistics(g):
                if not isinstance(g, int) or g > 0:
                    dve.wait_ge(f_ln, g)
                for t in range(GROUP):
                    ins = dve.bn_stats(FBN[:, t, :], XF[:, tile_at(g, t), :])
                ins.then_inc(f_bn, 1)

            def f_aggregate(g):
                for t in range(GROUP):
                    ins = dve.bn_aggr(FMV[:, t, :], FBN[:, t, :])
                ins.then_inc(f_stats, 1)

            def f_normalise(g):
                dve.wait_ge(f_ln, g + 1)
                if not isinstance(g, int) or g > 0:
                    dve.wait_ge(f_xT, g)
                for t in range(GROUP):
                    ins = dve.tensor_scalar(FXH[:, t:t + 1, :], XF[:, tile_at(g, t), :], FLN[:, 1, t:t + 1],
                                            FLN[:, 3, t:t + 1], ALU.mult, ALU.add)
                ins.then_inc(f_xhat, 1)

            def h_high(g):
                dve.wait_ge(f_hT, g + 1)
                dve.tensor_copy(FHHI[:, :], FH[:, :, :].rearrange("p a t -> p (a t)")).then_inc(f_hhi, 1)

            def high(g, layer, kb):
                dve.wait_ge(raw_ready, g * 8 + (4 * layer + kb + 1))
                dve.tensor_copy(HI[layer][:, kb, :], RAW[:, kb, :]).then_inc(hi_ready, 1)
                if kb % 2:
                    dve.wait_ge(hi_ready, g * 8 + (4 * layer + kb + 1))
                    dve.tensor_tensor(LO[layer][:, kb, :], RAW[:, kb, :], HI[layer][:, kb, :].bitcast(f32),
                                      ALU.subtract).then_inc(lo_odd, 1)

            def f_output(g):
                dve.wait_ge(y_back, g + 1)
                if not isinstance(g, int) or g > 0:
                    dve.wait_ge(out_stored, g * 16)
                dve.tensor_tensor(OUT[:, :, :], OT[:, :, :].rearrange("p a (t e) -> p (a t) e", e=EMB),
                                  XF[:, tile_at(g, 0, GROUP), :], ALU.add).then_inc(out_ready, 1)

            def f_group(g, first, more):
                if more:
                    f_statistics(g + 1)
                if more:
                    dve.wait_ge(f_bn, g + 2)
                high(g, 1, 0)
                if more:
                    f_aggregate(g + 1)
                    f_normalise(g + 1)
                if not first:
                    f_output(g - 1)
                high(g, 1, 1)
                if more:
                    h_high(g + 1)
                high(g, 1, 2)
                high(g, 1, 3)
                if more:
                    for kb in range(BLOCKS):
                        high(g + 1, 0, kb)

            dve.wait_ge(ffn_loaded, 48)
            dve.tensor_tensor(W0[:, :], U0[:, 0, :], U0[:, 1, :], ALU.subtract).then_inc(fw_ready, 1)
            dve.wait_ge(x1_ready, BATCHES)
            f_statistics(0)
            dve.wait_ge(f_bn, 1)
            f_aggregate(0)
            f_normalise(0)
            h_high(0)
            for kb in range(BLOCKS):
                high(0, 0, kb)
            f_group(0, True, True)
            with dve.Fori(1, GROUPS - 1) as g:
                f_group(g, False, True)
            f_group(GROUPS - 1, False, False)
            f_output(GROUPS - 1)

        @block.tensor
        def _(pe):
            pe.wait_ge(mod_loaded, 48)
            pe.wait_ge(silu_step, 3)
            for j in range(6):
                ins = pe.matmul(PB[:, j * BATCHES:(j + 1) * BATCHES], WMOD[:, j * EMB:(j + 1) * EMB],
                                SILU[:, 0, :], start=True, stop=True)
            ins.then_inc(mod_ready, 1)
            pe.wait_ge(w_loaded, 96)

            def turn_x(b):
                wait(pe, xhat_ready, b.count(1, 1))
                wait(pe, v_copied, b.count(1, 0))
                for t in range(TILES):
                    ins = pe.transpose(PA[:, t * LANES:(t + 1) * LANES], XH[:, t, :], EYE[:, :])
                ins.then_inc(xT_ready, 1)

            def project(b, w, ready, free, free_at):
                wait(pe, free, free_at)
                for s in range(2):
                    ins = pe.matmul(PA[:, s * SEQ:(s + 1) * SEQ], w[:, s, :], HT[:, :], start=True, stop=True)
                ins.then_inc(ready, 1)

            def project_v(b):
                wait(pe, turned_k, b.count(1, 1))
                wait(pe, o_gated, b.count(1, -3))
                for t in range(TILES):
                    ins = pe.matmul(PA[:, t * LANES:(t + 1) * LANES], HT[:, t * LANES:(t + 1) * LANES],
                                    WV[:, :], start=True, stop=True)
                ins.then_inc(v_ready, 1)

            def scores_for_max(b, h):
                base, n = 64 * (h % 2), h // 2
                if h == 0:
                    wait(pe, stack_ready[b.slot], b.in_slot(16 * STACK_DMAS))
                wait(pe, max_ready, b.count(HEADS, s1_bank_read(h)))
                rows = ST[b.slot][base:base + STACK, n, :, :]
                for t in range(TILES):
                    ins = pe.matmul(S1[s1_bank(h)][:, t, :], rows[:, 0, t * LANES:(t + 1) * LANES], rows[:, 1, :],
                                    start=True, stop=True)
                ins.then_inc(s1_ready, 1)

            def turn_max(b):
                wait(pe, mparts_ready, b.count(1, 1))
                wait(pe, y_normed, b.count(2, -2))
                if b.known == 0:
                    pe.wait_ge(mod_step, 1)
                    pe.wait_ge(eyeb_set, 1)
                for t in range(TILES):
                    ins = pe.transpose(MT_PSUM[:, t * LANES:(t + 1) * LANES],
                                       NPART[:, t, :], EYEB[:, :])
                ins.then_inc(mT_ready, 1)

            def shifted_scores(b, h):
                base, n = 64 * (h % 2), h // 2
                if h == 0:
                    wait(pe, mrows_ready[b.slot], b.in_slot(32))
                wait(pe, exp_ready, b.count(HEADS, h - 1))
                rows = ST[b.slot][base:base + SCORE_ROWS, n, :, :]
                for t in range(TILES):
                    ins = pe.matmul(S2[h % 2][:, t, :], rows[:, 1, t * LANES:(t + 1) * LANES], rows[:, 0, :],
                                    start=True, stop=True)
                ins.then_inc(s2_ready, 1)

            def weigh_values(b, quad, t):
                if t == 0:
                    wait(pe, exp_ready, b.count(HEADS, QUAD * quad + QUAD))
                    wait(pe, v_copied, b.count(1, 1))
                    wait(pe, ot_copied, b.count(2, quad // 2))
                for c in range(QUAD):
                    h = QUAD * quad + c
                    ins = pe.matmul(OT[32 * c:32 * c + 32, quad % 2, :], VS[b.slot][:, t, h, :],
                                    PT[:, h % (2 * QUAD), t, :], start=(t == 0), stop=(t == TILES - 1))
                if t == TILES - 1:
                    ins.then_inc(pv_ready, 1)

            def turn_y(b, t):
                if t == 0:
                    wait(pe, ot_copied, b.count(2, 2))
                    wait(pe, x1_ready, b.count(1, 0))
                else:
                    wait(pe, y_normed, b.count(2, 1))
                for q in range(HEADS // QUAD):
                    ins = pe.transpose(PB[:, q * LANES:(q + 1) * LANES], OTS[:, q, t * LANES:(t + 1) * LANES], EYE[:, :])
                ins.then_inc(y_turned, 1)

            def turn_y_back(b):
                wait(pe, y_normed, b.count(2, 2))
                wait(pe, mT_copied, b.capped(3))
                for t in range(TILES):
                    ins = pe.transpose(PB[:, t * LANES:(t + 1) * LANES], YN[:, t, :], EYE[:, :])
                ins.then_inc(yT_ready, 1)

            def project_out(b):
                wait(pe, yT_copied, b.count(1, 1))
                wait(pe, v_copied, b.capped(4))
                wait(pe, turned_k, b.capped(5))
                pe.matmul(PA[:, 0:SEQ], WO[:, :], YT[:, :], start=True, stop=True).then_inc(o_ready, 1)

            def turn_out(b):
                wait(pe, o_gated, b.count(1, 1))
                wait(pe, yT_copied, b.count(1, 1))
                for t in range(TILES):
                    ins = pe.transpose(PB[:, t * LANES:(t + 1) * LANES], OE[:, t * LANES:(t + 1) * LANES], EYE[:, :])
                ins.then_inc(o_turned, 1)

            def iteration(b):
                tail, prep = b.plus(-1), b.plus(3)
                for h in range(HEADS):
                    if b.exists():
                        shifted_scores(b, h)
                    m = b.plus(1 + h // LEAD)
                    if m.exists():
                        scores_for_max(m, (h + LEAD) % HEADS)
                    if tail.exists():
                        if h in (0, 1):
                            weigh_values(tail, 3, h)
                        if h == 3:
                            turn_y(tail, 0)
                        if h == 6:
                            turn_y(tail, 1)
                        if h == 11:
                            turn_y_back(tail)
                        if h == 13:
                            project_out(tail)
                        if h == 15:
                            turn_out(tail)
                    if b.exists() and h in (4, 5, 8, 9, 12, 14):
                        weigh_values(b, (h - 4) // QUAD, int(h not in (4, 8, 12)))
                    if b.plus(2).exists() and h == 2:
                        project_v(b.plus(2))
                    if prep.exists():
                        if h == 5:
                            turn_x(prep)
                        if h == 7:
                            project(prep, WQ, q_ready, hT_ready, prep.count(1, 1))
                        if h == 10:
                            project(prep, WK, k_ready, turned_q, prep.count(1, 1))
                    if b.plus(1).exists() and h == 9:
                        turn_max(b.plus(1))

            MT_PSUM = PB[:, 0:SEQ // 2].bitcast(bf16)

            def prepare(b):
                turn_x(b)
                project(b, WQ, q_ready, hT_ready, b.count(1, 1))
                project(b, WK, k_ready, turned_q, b.count(1, 1))

            prepare(Batch(0, 0))
            project_v(Batch(0, 0))
            prepare(Batch(0, 1))
            project_v(Batch(0, 1))
            for h in range(HEADS):
                scores_for_max(Batch(0, 0), h)
            prepare(Batch(0, 2))
            turn_max(Batch(0, 0))
            for h in range(LEAD):
                scores_for_max(Batch(0, 1), h)
            iteration(Batch(0, 0))
            with pe.Fori(0, 3) as turn:
                for j in range(RING):
                    iteration(Batch(turn, 1 + j))
            for b in range(13, BATCHES + 1):
                iteration(Batch(0, b))

            def f_turn(g):
                pe.wait_ge(f_xhat, g + 1)
                if not isinstance(g, int) or g > 0:
                    pe.wait_ge(f_hT, g)
                for t in range(GROUP):
                    ins = pe.transpose(PA[:, t * LANES:(t + 1) * LANES], FXH[:, t, :], EYE[:, :])
                ins.then_inc(f_xT, 1)

            def f_layer0(g):
                pe.wait_ge(f_hhi, g + 1)
                pe.wait_ge(f_hlo, g + 1)
                for f in range(BLOCKS):
                    if not isinstance(g, int) or g > 0:
                        pe.wait_ge(raw_ready, g * 8 + (f - 3))
                    bank = (S1 + S2)[f][:, :, :].rearrange("p a t -> p (a t)")
                    w = W0[:, f * LANES:(f + 1) * LANES]
                    pe.matmul(bank, w, FHHI[:, :], start=True, stop=False)
                    pe.matmul(bank, w, FHLO[:, :], start=False, stop=True).then_inc(block_ready, 1)

            def f_layer1(g, f):
                pe.wait_ge(raw_ready, g * 8 + (f + 1))
                bank = (S1 + S2)[f][:, :, :].rearrange("p a t -> p (a t)")
                for kb in range(BLOCKS):
                    if f == 0:
                        pe.wait_ge(hi_ready, g * 8 + (kb + 1))
                        pe.wait_ge(lo_odd if kb % 2 else lo_even, g * 4 + (kb // 2 + 1))
                    w = W1[:, kb, f * LANES:(f + 1) * LANES]
                    pe.matmul(bank, w, HI[0][:, kb, :], start=(kb == 0), stop=False)
                    ins = pe.matmul(bank, w, LO[0][:, kb, :], start=False, stop=(kb == BLOCKS - 1))
                ins.then_inc(block_ready, 1)

            def f_layer2(g):
                if not isinstance(g, int) or g > 0:
                    pe.wait_ge(y_gated, g)
                for kb in range(BLOCKS):
                    pe.wait_ge(hi_ready, g * 8 + (kb + 5))
                    pe.wait_ge(lo_odd if kb % 2 else lo_even, g * 4 + (kb // 2 + 3))
                    pe.matmul(PB[:, :], W2[:, kb, :], HI[1][:, kb, :], start=(kb == 0), stop=False)
                    ins = pe.matmul(PB[:, :], W2[:, kb, :], LO[1][:, kb, :], start=False, stop=(kb == BLOCKS - 1))
                ins.then_inc(y_ready, 1)

            def f_turn_back(g):
                pe.wait_ge(y_gated, g + 1)
                if not isinstance(g, int) or g > 0:
                    pe.wait_ge(out_ready, g)
                for t in range(GROUP):
                    ins = pe.transpose(OT[:, t // 2, (t % 2) * LANES:(t % 2 + 1) * LANES],
                                       FY[:, t // 2, (t % 2) * LANES:(t % 2 + 1) * LANES], EYE[:, :])
                ins.then_inc(y_back, 1)

            def f_group(g, first, more):
                f_layer1(g, 0)
                if not first:
                    f_turn_back(g - 1)
                f_layer1(g, 1)
                if more:
                    f_turn(g + 1)
                f_layer1(g, 2)
                f_layer1(g, 3)
                if more:
                    f_layer0(g + 1)
                f_layer2(g)

            pe.wait_ge(o_gated, BATCHES)
            pe.wait_ge(x1_ready, BATCHES)
            pe.wait_ge(ot_copied, 2 * BATCHES)
            pe.wait_ge(max_ready, HEADS * BATCHES)
            pe.wait_ge(exp_ready, HEADS * BATCHES)
            pe.wait_ge(fw_ready, 3)
            f_turn(0)
            f_layer0(0)
            f_group(0, True, True)
            with pe.Fori(1, GROUPS - 1) as g:
                f_group(g, False, True)
            f_group(GROUPS - 1, False, False)
            f_turn_back(GROUPS - 1)


def rope_table():
    i = np.arange(HEAD_DIM // 2, dtype=np.float32)
    rate = np.power(np.float32(10000.0), np.float32(2.0) * i / np.float32(HEAD_DIM))
    theta = np.arange(SEQ, dtype=np.float32)[:, None] * rate[None, :]
    theta = theta.astype(np.float64)
    cos, sin = np.cos(theta), np.sin(theta)
    position = np.arange(SEQ).reshape(LANES, TILES).T.reshape(-1)
    table = np.zeros((LANES, 2, 2, SEQ), np.float64)
    for p in range(LANES):
        d = p % 64 // (HEADS // 2)
        for s, scale in enumerate((1.0 / np.sqrt(HEAD_DIM), 1.0)):
            table[p, s, 0] = cos[position, d // 2] * scale
            table[p, s, 1] = sin[position, d // 2] * scale * (1 if d % 2 else -1)
    return table.reshape(LANES, 2, 2 * SEQ).astype(np.float32)


def kernel(**inputs):
    import concourse.bacc as _bacc
    from concourse.bass_utils import run_bass_kernel_spmd as _run

    a = {k: np.asarray(v) for k, v in inputs.items()}

    def plain_and_swapped(w):
        w = w.reshape(HEADS // 2, 2, HEAD_DIM // 2, 2, EMB)
        both = np.stack([w, w[:, :, :, ::-1]], 0).reshape(2, HEADS // 2, 2, HEAD_DIM, EMB)
        return both.transpose(4, 0, 2, 3, 1).reshape(EMB, 2, EMB)

    arrays = {
        "x": a["L0_attn_x"],
        "wq": plain_and_swapped(a["L0_attn_w_q"]),
        "wk": plain_and_swapped(a["L0_attn_w_k"]),
        "wv": a["L0_attn_w_v"].T,
        "wo": a["L0_attn_w_o"].T,
        "rope": rope_table(),
        "eye": np.eye(LANES, dtype=np.float32),
        "c_t": a["L0_c"].T,
        "wmod": a["L0_wmod"],
        "k0": a["L0_ffn_k0"],
        "k1": a["L0_ffn_k1"],
        "k2": a["L0_ffn_k2"],
        "scales": np.stack([a["L0_ffn_s0"], a["L0_ffn_s1"], a["L0_ffn_s2"]]).reshape(1, 3),
    }
    arrays = {k: np.ascontiguousarray(v) for k, v in arrays.items()}
    nc = _bacc.Bacc("TRN2", target_bir_lowering=False, num_devices=1)
    args = [nc.dram_tensor(f"in_{k}", v.shape, mybir.dt.from_np(v.dtype), kind="ExternalInput").ap()
            for k, v in arrays.items()]
    out = nc.dram_tensor("out", (BATCHES, SEQ, EMB), mybir.dt.float32, kind="ExternalOutput").ap()
    adaln_block(nc, *args, out)
    r = _run(nc, [{f"in_{k}": v for k, v in arrays.items()}], core_ids=[0])
    return r.results[0]["out"]
```

```python
import concourse.bass as bass
from concourse import mybir
from contextlib import ExitStack
import numpy as np

BATCHES, SEQ, EMB, HEADS = 16, 256, 128, 16
HEAD_DIM = EMB // HEADS
HIDDEN = 512
LANES = 128
TILES = SEQ // LANES
PARTS = 3
PRODUCTS = [(0, 0), (0, 1), (0, 2), (1, 0), (1, 1), (2, 0)]
STACK = len(PRODUCTS) * HEAD_DIM
SCORE_ROWS = STACK + PARTS
MCOLS = PARTS * HEADS
RING = 4
QUAD = 4
EPS = 1e-5
GROUP = 4
GROUPS = BATCHES * TILES // GROUP
BLOCKS = HIDDEN // LANES
LEAD = HEADS // 2


class Batch:

    def __init__(self, turn, k):
        self.turn, self.k = turn, k
        self.slot, self.pair = k % RING, k % 2
        self.known = k if isinstance(turn, int) else None

    def plus(self, d):
        return Batch(self.turn, self.k + d)

    def exists(self):
        return self.known is None or 0 <= self.known < BATCHES

    def number(self):
        return self.turn * RING + self.k

    def count(self, each, extra):
        return self.turn * (RING * each) + (self.k * each + extra)

    def in_slot(self, each):
        return self.turn * each + (self.k // RING + 1) * each

    def capped(self, ahead):
        n = self.count(1, ahead)
        return min(n, BATCHES) if isinstance(n, int) else n


def wait(engine, sem, value):
    if not isinstance(value, int) or value > 0:
        engine.wait_ge(sem, value)


def adaln_block(nc: bass.Bass, x, wq, wk, wv, wo, rope, eye, c_t, wmod, k0, k1, k2, scales, out):
    f32, f32r, bf16, u8 = mybir.dt.float32, mybir.dt.float32r, mybir.dt.bfloat16, mybir.dt.uint8
    ALU, ACT, AX = mybir.AluOpType, mybir.ActivationFunctionType, mybir.AxisListType
    x_v = x.rearrange("b (p t) e -> p b t e", t=TILES)
    out_v = out.rearrange("b (p t) e -> p b t e", t=TILES)

    ctx = ExitStack()
    with ctx:
        def sb(name, shape, dt=f32):
            return ctx.enter_context(nc.sbuf_tensor(name, shape, dt))

        def ps(name, shape):
            return ctx.enter_context(nc.psum_tensor(name, shape, f32))

        def sem(name):
            return ctx.enter_context(nc.semaphore(name))

        X = sb("X", [LANES, BATCHES, TILES, EMB])
        WQ = sb("WQ", [EMB, 2, EMB])
        WK = sb("WK", [EMB, 2, EMB])
        WV = sb("WV", [EMB, EMB])
        WO = sb("WO", [EMB, EMB])
        ROPE = sb("ROPE", [LANES, 2, 2 * SEQ])
        EYE = sb("EYE", [LANES, LANES])
        EYEB = sb("EYEB", [LANES, LANES], bf16)
        CT = sb("CT", [EMB, BATCHES])
        SILU = sb("SILU", [EMB, 3, BATCHES])
        WMOD = sb("WMOD", [EMB, 6 * EMB])
        MOD = sb("MOD", [EMB, 6, BATCHES])
        GATE = sb("GATE", [EMB, 4, 2, BATCHES])
        SCALE = sb("SCALE", [LANES, 3])
        SIGN = sb("SIGN", [LANES, 2])
        SIGN2 = sb("SIGN2", [LANES, 2, 2])
        SIZE = sb("SIZE", [LANES, 5])
        BN = sb("BN", [LANES, TILES, 6])
        MEANVAR = sb("MEANVAR", [LANES, 2, TILES, 2])
        CONST = sb("CONST", [LANES, 3, GROUP])
        LN = sb("LN", [LANES, 4, TILES])
        XH = sb("XH", [LANES, TILES, EMB])
        HT = sb("HT", [EMB, SEQ])
        TURNED = sb("TURNED", [LANES, 2, 2 * SEQ])
        QK = sb("QK", [LANES, 2, SEQ])
        REST = sb("REST", [LANES, 2, SEQ])
        QKP = sb("QKP", [LANES, 2, PARTS, SEQ], bf16)
        ST = [sb(f"ST{r}", [LANES, HEADS // 2, 2, SEQ], bf16) for r in range(RING)]
        VS = [sb(f"VS{r}", [LANES, TILES, HEADS, 32]) for r in range(RING)]
        NMAX = sb("NMAX", [LANES, 2, TILES, 2, HEADS // 2])
        NREST = sb("NREST", [LANES, TILES, 2, HEADS // 2])
        NPART = sb("NPART", [LANES, TILES, LANES], bf16)
        MROW = sb("MROW", [MCOLS, SEQ], bf16)
        PT = sb("PT", [LANES, 2 * QUAD, TILES, SEQ])
        OTS = sb("OTS", [LANES, HEADS // QUAD, SEQ])
        RDEN = sb("RDEN", [LANES, TILES, HEADS])
        YN = sb("YN", [LANES, TILES, EMB])
        YT = sb("YT", [EMB, SEQ])
        OE = sb("OE", [EMB, SEQ])
        U0 = sb("U0", [EMB, 2, HIDDEN], u8)
        U1 = sb("U1", [LANES, BLOCKS, HIDDEN], u8)
        U2 = sb("U2", [LANES, BLOCKS, EMB], u8)
        W0 = sb("W0", [EMB, HIDDEN], f32r)
        W1 = sb("W1", [LANES, BLOCKS, HIDDEN], f32r)
        W2 = sb("W2", [LANES, BLOCKS, EMB], f32r)
        FBN = sb("FBN", [LANES, GROUP, 6])
        FMV = sb("FMV", [LANES, GROUP, 2])
        FLN = sb("FLN", [LANES, 4, GROUP])
        FXH = sb("FXH", [LANES, GROUP, EMB])
        FH = sb("FH", [EMB, 2, SEQ])
        WDIFF = sb("WDIFF", [EMB, HIDDEN])
        FHHI = sb("FHHI", [EMB, 2 * SEQ], f32r)
        FHLO = sb("FHLO", [EMB, 2 * SEQ], f32r)
        HI = [sb(f"HI{n}", [LANES, BLOCKS, GROUP * LANES], f32r) for n in range(2)]
        LO = [sb(f"LO{n}", [LANES, BLOCKS, GROUP * LANES], f32r) for n in range(2)]
        FY = sb("FY", [EMB, 2, SEQ])
        OUT = sb("OUT", [LANES, GROUP, EMB])

        S1 = [ps(f"S1{n}", [LANES, TILES, SEQ]) for n in range(3)]
        S2 = [ps(f"S2{n}", [LANES, TILES, SEQ]) for n in range(2)]
        OT = ps("OT", [LANES, 2, SEQ])
        PA = ps("PA", [LANES, 2 * SEQ])
        PB = ps("PB", [LANES, 2 * SEQ])
        MT_PSUM = PB[:, 0:SEQ // 2].bitcast(bf16)
        FBANKS = S1 + S2

        x_loaded = [sem(f"x_loaded{n}") for n in range(4)]
        w_loaded = sem("w_loaded")
        mod_loaded = sem("mod_loaded")
        ffn_loaded = sem("ffn_loaded")
        ones_set, eyeb_set = sem("ones_set"), sem("eyeb_set")
        c_exp, silu_step, mod_ready, mod_step = sem("c_exp"), sem("silu_step"), sem("mod_ready"), sem("mod_step")
        bn_ready, stats_ready, ln_step, ln_ready = sem("bn_ready"), sem("stats_ready"), sem("ln_step"), sem("ln_ready")
        xhat_ready, xT_ready, hT_ready = sem("xhat_ready"), sem("xT_ready"), sem("hT_ready")
        q_ready, k_ready, v_ready, v_copied = sem("q_ready"), sem("k_ready"), sem("v_ready"), sem("v_copied")
        turned_q, turned_k, sum_ready = sem("turned_q"), sem("turned_k"), sem("sum_ready")
        part1, rest_ready, part2, part3 = sem("part1"), sem("rest_ready"), sem("part2"), sem("part3")
        stack_ready = [sem(f"stack_ready{n}") for n in range(RING)]
        mrows_ready = [sem(f"mrows_ready{n}") for n in range(RING)]
        s1_ready, max_ready, mpart_step, mparts_ready = sem("s1_ready"), sem("max_ready"), sem("mpart_step"), sem("mparts_ready")
        mT_ready, mT_copied = sem("mT_ready"), sem("mT_copied")
        s2_ready, exp_ready, pv_ready, ot_copied = sem("s2_ready"), sem("exp_ready"), sem("pv_ready"), sem("ot_copied")
        y_turned, rden_ready, y_normed = sem("y_turned"), sem("rden_ready"), sem("y_normed")
        yT_ready, yT_copied, o_ready, o_gated = sem("yT_ready"), sem("yT_copied"), sem("o_ready"), sem("o_gated")
        o_turned, x1_ready = sem("o_turned"), sem("x1_ready")
        fw_ready = sem("fw_ready")
        f_bn, f_stats, f_ln_step, f_ln = sem("f_bn"), sem("f_stats"), sem("f_ln_step"), sem("f_ln")
        f_xhat, f_xT, f_hT, f_hhi, f_hlo = sem("f_xhat"), sem("f_xT"), sem("f_hT"), sem("f_hhi"), sem("f_hlo")
        sign_step, wdiff_ready = sem("sign_step"), sem("wdiff_ready")
        block_ready, hi_ready, lo_ready = sem("block_ready"), sem("hi_ready"), sem("lo_ready")
        y_ready, y_gated, y_back, out_ready, out_stored = (sem("y_ready"), sem("y_gated"), sem("y_back"),
                                                           sem("out_ready"), sem("out_stored"))

        STACK_DMAS = 2 * len(PRODUCTS)
        X_CHUNKS = [0, 1, 4, 8, 16]

        def s1_bank(h):
            return 1 if h == HEADS - 1 else h % 3

        def s1_bank_read(h):
            before = [g for g in range(h - HEADS, h) if s1_bank(g % HEADS) == s1_bank(h)]
            return before[-1] + 1

        def x_chunk(b):
            return max(n for n in range(4) if X_CHUNKS[n] <= b)

        def layer_bank(g, layer, f):
            if layer == 0:
                f = (1, 2, 0, 1)[f] if isinstance(g, int) and g == 0 else (4, 0, 1, 2)[f]
            return FBANKS[f][:, :, :].rearrange("p a t -> p (a t)")

        block = ctx.enter_context(nc.Block())

        @block.sync
        def _(sp):
            for n in range(4):
                sp.dma_start(X[:, X_CHUNKS[n]:X_CHUNKS[n + 1]], x_v[:, X_CHUNKS[n]:X_CHUNKS[n + 1]]).then_inc(x_loaded[n], 16)
                if n == 0:
                    sp.dma_start(CT[:, :], c_t).then_inc(mod_loaded, 16)
                    sp.dma_start(WMOD[:, :], wmod).then_inc(mod_loaded, 16)
                    sp.dma_start(SCALE[:, :], scales.to_broadcast([LANES, 3])).then_inc(mod_loaded, 16)
                    sp.dma_start(EYE[:, :], eye).then_inc(w_loaded, 16)
                    for dst, src in ((WQ, wq), (WK, wk), (ROPE, rope)):
                        sp.dma_start(dst[:, :, :], src).then_inc(w_loaded, 16)
                    for dst, src in ((WV, wv), (WO, wo)):
                        sp.dma_start(dst[:, :], src).then_inc(w_loaded, 16)
            sp.dma_start(U0[:, :, :], k0.rearrange("(s p) n -> p s n", s=2)).then_inc(ffn_loaded, 16)
            sp.dma_start(U1[:, :, :], k1.rearrange("(s p) n -> p s n", s=BLOCKS)).then_inc(ffn_loaded, 16)
            sp.dma_start(U2[:, :, :], k2.rearrange("(s p) n -> p s n", s=BLOCKS)).then_inc(ffn_loaded, 16)

            def stack(b, parts, last):
                wait(sp, parts, b.count(1, 1))
                if b.known is not None and b.known < RING and last == 0:
                    sp.wait_ge(ones_set, b.known + 1)
                for j, (qp, kp) in enumerate(PRODUCTS):
                    for half in range(2 if max(qp, kp) == last else 0):
                        row, src = 64 * half + HEAD_DIM * j, QKP[64 * half:64 * half + 64, :, :, :]
                        src = src.rearrange("p a c t -> p (a c) t")[:, qp:PARTS + kp + 1:PARTS + kp - qp, :]
                        sp.dma_start(ST[b.slot][row:row + HEAD_DIM, :, :, :], src).then_inc(stack_ready[b.slot], 16)

            def max_rows(b):
                wait(sp, mT_copied, b.count(1, 1))
                for half in range(2):
                    row, n = 64 * half + STACK, PARTS * HEADS // 2
                    sp.dma_start(ST[b.slot][row:row + PARTS, :, 0, :],
                                 MROW[half * n:(half + 1) * n, :]).then_inc(mrows_ready[b.slot], 16)

            def whole_stack(b):
                for last, parts in enumerate((part1, part2, part3)):
                    stack(b, parts, last)

            def iteration(b):
                if b.plus(1).exists():
                    max_rows(b.plus(1))
                if b.plus(3).exists():
                    whole_stack(b.plus(3))

            whole_stack(Batch(0, 0))
            whole_stack(Batch(0, 1))
            max_rows(Batch(0, 0))
            whole_stack(Batch(0, 2))
            iteration(Batch(0, 0))
            with sp.Fori(0, 3) as turn:
                for j in range(RING):
                    iteration(Batch(turn, 1 + j))
            for b in range(13, BATCHES):
                iteration(Batch(0, b))

            for g in range(GROUPS):
                sp.wait_ge(out_ready, g + 1)
                sp.dma_start(out_v[:, 2 * g:2 * g + 2, :, :], OUT[:, :, :]).then_inc(out_stored, 16)
            sp.wait_ge(out_stored, 16 * GROUPS)

        @block.gpsimd
        def _(pool):
            for n, value in enumerate((-0.5, EPS, -1.0)):
                pool.memset(CONST[:, n, :], value)
            pool.memset(NPART[:, :, :], 0.0)
            def constants(r):
                pool.memset(ST[r][:, :, 1, :], 1.0)
                pool.memset(VS[r][:, :, :, HEAD_DIM + 1:32], 0.0)
                pool.memset(VS[r][:, :, :, HEAD_DIM:HEAD_DIM + 1], 1.0).then_inc(ones_set, 1)

            def layer_norm(b):
                wait(pool, stats_ready, b.count(1, 1))
                wait(pool, xhat_ready, b.count(1, 0))
                mv = MEANVAR[:, b.pair]
                pool.tensor_tensor(LN[:, 0, :], mv[:, :, 1], CONST[:, 1, 0:TILES], ALU.add).then_inc(ln_step, 1)
                wait(pool, ln_step, b.count(3, 1))
                pool.tensor_tensor(LN[:, 1, :], LN[:, 0, :], CONST[:, 0, 0:TILES], ALU.pow).then_inc(ln_step, 1)
                wait(pool, ln_step, b.count(3, 2))
                pool.tensor_tensor(LN[:, 2, :], mv[:, :, 0], LN[:, 1, :], ALU.mult).then_inc(ln_step, 1)
                wait(pool, ln_step, b.count(3, 3))
                pool.tensor_tensor(LN[:, 3, :], LN[:, 2, :], CONST[:, 2, 0:TILES], ALU.mult).then_inc(ln_ready, 1)

            def rotate_and_split(b):
                wait(pool, turned_k, b.count(1, 1))
                wait(pool, part3, b.count(1, 0))
                pool.tensor_tensor(QK[:, :, :], TURNED[:, :, 0:SEQ], TURNED[:, :, SEQ:2 * SEQ],
                                   ALU.add).then_inc(sum_ready, 1)
                if b.k > 0 or b.known is None:
                    before = b.plus(-1)
                    wait(pool, stack_ready[before.slot], before.in_slot(16 * STACK_DMAS))
                wait(pool, s2_ready, b.count(HEADS, -(RING - 1) * HEADS))
                pool.tensor_tensor(QKP[:, :, 0, :], TURNED[:, :, 0:SEQ], TURNED[:, :, SEQ:2 * SEQ],
                                   ALU.add).then_inc(part1, 1)
                wait(pool, sum_ready, b.count(1, 1))
                wait(pool, part1, b.count(1, 1))
                pool.tensor_tensor(QKP[:, :, 1, :], QK[:, :, :], QKP[:, :, 0, :], ALU.subtract).then_inc(part2, 1)
                pool.tensor_tensor(REST[:, :, :], QK[:, :, :], QKP[:, :, 0, :], ALU.subtract).then_inc(rest_ready, 1)
                wait(pool, rest_ready, b.count(1, 1))
                wait(pool, part2, b.count(1, 1))
                pool.tensor_tensor(QKP[:, :, 2, :], REST[:, :, :], QKP[:, :, 1, :], ALU.subtract).then_inc(part3, 1)

            def iteration(b):
                if b.plus(3).exists():
                    layer_norm(b.plus(3))
                    rotate_and_split(b.plus(3))

            constants(0)
            pool.wait_ge(ones_set, 1)
            for n in range(3):
                layer_norm(Batch(0, n))
                constants(n + 1)
                rotate_and_split(Batch(0, n))
            iteration(Batch(0, 0))
            with pool.Fori(0, 3) as turn:
                for j in range(RING):
                    iteration(Batch(turn, 1 + j))

            pool.wait_ge(ffn_loaded, 48)
            pool.wait_ge(sign_step, 5)
            pool.tensor_scalar(W1[:, :, :], U1[:, :, :], SIGN2[:, 0, 1:2], SIGN2[:, 1, 1:2],
                               ALU.mult, ALU.add).then_inc(fw_ready, 1)
            pool.tensor_scalar(W2[:, :, :], U2[:, :, :], 2.0, -1.0, ALU.mult, ALU.add).then_inc(fw_ready, 1)

            def f_norm(g):
                pool.wait_ge(f_stats, g + 1)
                if not isinstance(g, int) or g > 0:
                    pool.wait_ge(f_xhat, g)
                pool.tensor_tensor(FLN[:, 0, :], FMV[:, :, 1], CONST[:, 1, :], ALU.add).then_inc(f_ln_step, 1)
                pool.wait_ge(f_ln_step, g * 3 + 1)
                pool.tensor_tensor(FLN[:, 1, :], FLN[:, 0, :], CONST[:, 0, :], ALU.pow).then_inc(f_ln_step, 1)
                pool.wait_ge(f_ln_step, g * 3 + 2)
                pool.tensor_tensor(FLN[:, 2, :], FMV[:, :, 0], FLN[:, 1, :], ALU.mult).then_inc(f_ln_step, 1)
                pool.wait_ge(f_ln_step, g * 3 + 3)
                pool.tensor_tensor(FLN[:, 3, :], FLN[:, 2, :], CONST[:, 2, :], ALU.mult).then_inc(f_ln, 1)

            def h_low(g):
                pool.wait_ge(f_hhi, g + 1)
                pool.tensor_tensor(FHLO[:, :], FH[:, :, :].rearrange("p a t -> p (a t)"),
                                   FHHI[:, :].bitcast(f32), ALU.subtract).then_inc(f_hlo, 1)

            for g in range(2):
                f_norm(g)
                h_low(g)
            with pool.Fori(2, GROUPS) as g:
                f_norm(g)
                h_low(g)

        @block.scalar
        def _(act):
            act.wait_ge(mod_loaded, 48)
            act.activation(SILU[:, 0, :], CT[:, :], ACT.Exp, scale=-1.0).then_inc(c_exp, 1)

            def normalise(b):
                wait(act, ln_ready, b.count(1, 1))
                wait(act, xT_ready, b.count(1, 0))
                for t in range(TILES):
                    ins = act.activation(XH[:, t, :], X[:, at(b), t, :], ACT.Identity,
                                         bias=LN[:, 3, t:t + 1], scale=LN[:, 1, t:t + 1])
                ins.then_inc(xhat_ready, 1)

            def at(b):
                return b.known if b.known is not None else bass.ds(b.number(), 1)

            def col(tile, j, b):
                n = b.number() if b.known is None else b.known
                return tile[:, j, bass.ds(n, 1)] if b.known is None else tile[:, j, n:n + 1]

            def modulate(b):
                wait(act, xT_ready, b.count(1, 1))
                if b.known == 0:
                    act.wait_ge(mod_step, 6)
                act.activation(HT[:, :], PA[:, 0:SEQ], ACT.Identity, bias=col(MOD, 0, b),
                               scale=col(MOD, 1, b)).then_inc(hT_ready, 1)

            def copy_v(b):
                wait(act, v_ready, b.count(1, 1))
                wait(act, pv_ready, b.count(4, -4 * (RING - 1)))
                if b.known is not None and b.known < RING:
                    act.wait_ge(ones_set, b.known + 1)
                act.activation(VS[b.slot][:, :, :, 0:HEAD_DIM],
                               PA[:, 0:SEQ].rearrange("p (t h d) -> p t h d", t=TILES, h=HEADS),
                               ACT.Copy).then_inc(v_copied, 1)

            def exps(b, h):
                wait(act, s2_ready, b.count(HEADS, h + 1))
                if h % QUAD == 0:
                    wait(act, pv_ready, b.count(4, h // QUAD - 1))
                act.activation(PT[:, h % (2 * QUAD), :, :], S2[h % 2][:, :, :], ACT.Exp).then_inc(exp_ready, 1)

            def copy_ot(b, half):
                wait(act, pv_ready, b.count(4, 2 * half + 2))
                wait(act, y_turned, b.count(2, 0))
                act.activation(OTS[:, 2 * half:2 * half + 2, :], OT[:, :, :],
                               ACT.Copy).then_inc(ot_copied, 1)

            def copy_yt(b):
                wait(act, yT_ready, b.count(1, 1))
                wait(act, o_ready, b.count(1, 0))
                act.activation(YT[:, :], PB[:, 0:SEQ], ACT.Copy).then_inc(yT_copied, 1)

            def copy_mt(b):
                wait(act, mT_ready, b.count(1, 1))
                if b.k > 0 or b.known is None:
                    before = b.plus(-1)
                    wait(act, mrows_ready[before.slot], before.in_slot(32))
                act.activation(MROW[:, :], MT_PSUM[0:MCOLS, :], ACT.Copy).then_inc(mT_copied, 1)

            def gate(b):
                wait(act, o_ready, b.count(1, 1))
                wait(act, o_turned, b.count(1, 0))
                act.activation(OE[:, :], PA[:, 0:SEQ], ACT.Identity, scale=col(MOD, 2, b)).then_inc(o_gated, 1)

            def iteration(b):
                tail, prep = b.plus(-1), b.plus(3)
                for h in range(HEADS):
                    if b.exists():
                        exps(b, h)
                    if tail.exists():
                        if h == 1:
                            copy_ot(tail, 1)
                        if h == 11:
                            copy_yt(tail)
                        if h == 13:
                            gate(tail)
                    if b.plus(2).exists() and h == 2:
                        copy_v(b.plus(2))
                    if prep.exists():
                        if h == 3:
                            normalise(prep)
                        if h == 5:
                            modulate(prep)
                    if b.exists() and h == 9:
                        copy_ot(b, 0)
                    if b.known == BATCHES - 1 and h == 6:
                        f_mod(0)
                    if b.known == BATCHES - 1 and h in (9, 10, 12, 14):
                        f_relu(0, 0, (9, 10, 12, 14).index(h))
                    if b.plus(1).exists() and h == 9:
                        copy_mt(b.plus(1))

            for n in range(3):
                normalise(Batch(0, n))
                modulate(Batch(0, n))
                if n < 2:
                    copy_v(Batch(0, n))
            copy_mt(Batch(0, 0))
            iteration(Batch(0, 0))
            with act.Fori(0, 3) as turn:
                for j in range(RING):
                    iteration(Batch(turn, 1 + j))
            for b in range(13, BATCHES - 1):
                iteration(Batch(0, b))

            def f_mod(g):
                act.wait_ge(f_xT, g + 1)
                if not isinstance(g, int) or g > 0:
                    act.wait_ge(f_hlo, g)
                for u in range(2):
                    n = g * 2 + u
                    c = slice(n, n + 1) if isinstance(g, int) else bass.ds(n, 1)
                    ins = act.activation(FH[:, u, :], PA[:, u * SEQ:(u + 1) * SEQ], ACT.Identity,
                                         bias=MOD[:, 3, c], scale=MOD[:, 4, c])
                ins.then_inc(f_hT, 1)

            def f_relu(g, layer, kb):
                act.wait_ge(block_ready, g * 8 + (4 * layer + kb + 1))
                act.activation(HI[layer][:, kb, :], layer_bank(g, layer, kb), ACT.Relu).then_inc(hi_ready, 1)

            def f_gate(g):
                act.wait_ge(y_ready, g + 1)
                if not isinstance(g, int) or g > 0:
                    act.wait_ge(y_back, g)
                for u in range(2):
                    n = g * 2 + u
                    c = slice(n, n + 1) if isinstance(g, int) else bass.ds(n, 1)
                    ins = act.activation(FY[:, u, :], PB[:, u * SEQ:(u + 1) * SEQ], ACT.Identity,
                                         scale=MOD[:, 5, c])
                ins.then_inc(y_gated, 1)

            def f_group(g, more):
                f_relu(g, 1, 0)
                if more:
                    f_mod(g + 1)
                f_relu(g, 1, 1)
                f_relu(g, 1, 2)
                f_relu(g, 1, 3)
                if more:
                    for kb in range(BLOCKS):
                        f_relu(g + 1, 0, kb)
                f_gate(g)

            last = Batch(0, BATCHES - 1)
            iteration(last)
            copy_ot(last, 1)
            f_mod(1)
            f_relu(0, 1, 0)
            f_relu(0, 1, 1)
            copy_yt(last)
            f_relu(0, 1, 2)
            gate(last)
            f_relu(0, 1, 3)
            for kb in range(BLOCKS):
                f_relu(1, 0, kb)
            f_gate(0)
            with act.Fori(1, GROUPS - 1) as g:
                f_group(g, True)
            f_group(GROUPS - 1, False)

        @block.vector
        def _(dve):
            dve.wait_ge(c_exp, 1)
            dve.tensor_scalar(SILU[:, 1, :], SILU[:, 0, :], 1.0, None, ALU.add).then_inc(silu_step, 1)
            dve.wait_ge(silu_step, 1)
            dve.reciprocal(SILU[:, 2, :], SILU[:, 1, :]).then_inc(silu_step, 1)
            dve.wait_ge(silu_step, 2)
            dve.tensor_tensor(SILU[:, 0, :], SILU[:, 2, :], CT[:, :], ALU.mult).then_inc(silu_step, 1)
            dve.wait_ge(w_loaded, 96)
            dve.tensor_copy(EYEB[:, :], EYE[:, :]).then_inc(eyeb_set, 1)

            def at(b):
                return b.known if b.known is not None else bass.ds(b.number(), 1)

            def statistics(b):
                if b.known is not None and b.known < 4:
                    dve.wait_ge(x_loaded[x_chunk(b.known)], 16)
                wait(dve, stats_ready, b.count(1, 0))
                wait(dve, ln_ready, b.count(1, -1))
                for t in range(TILES):
                    dve.bn_stats(BN[:, t, :], X[:, at(b), t, :]).then_inc(bn_ready, 1)

            def aggregate(b):
                for t in range(TILES):
                    ins = dve.bn_aggr(MEANVAR[:, b.pair, t, :], BN[:, t, :])
                ins.then_inc(stats_ready, 1)

            def modulation():
                dve.wait_ge(mod_ready, 1)
                dve.tensor_copy(MOD[:, :, :], PB[:, 0:6 * BATCHES].rearrange("p (j b) -> p j b", j=6)).then_inc(mod_step, 1)
                dve.wait_ge(mod_step, 1)
                dve.tensor_scalar(MOD[:, 1:5:3, :], MOD[:, 1:5:3, :], 1.0, None, ALU.add)
                dve.tensor_scalar(GATE[:, 0], MOD[:, 2:6:3, :], -1.0, None, ALU.mult)
                dve.tensor_scalar(GATE[:, 1], MOD[:, 2:6:3, :], 0.0, 2.0, ALU.is_ge, ALU.mult).then_inc(mod_step, 1)
                dve.wait_ge(mod_step, 2)
                dve.tensor_tensor(GATE[:, 2], MOD[:, 2:6:3, :], GATE[:, 0], ALU.max).then_inc(mod_step, 1)
                dve.wait_ge(mod_step, 3)
                dve.tensor_scalar(GATE[:, 3], GATE[:, 2], 0.25, None, ALU.max)
                dve.tensor_scalar(GATE[:, 0], GATE[:, 1], -1.0, None, ALU.add).then_inc(mod_step, 1)
                dve.wait_ge(mod_step, 4)
                dve.tensor_tensor(MOD[:, 2:6:3, :], GATE[:, 0], GATE[:, 3], ALU.mult).then_inc(mod_step, 1)
                dve.wait_ge(mod_step, 5)
                dve.tensor_scalar(SIGN[:, :], SCALE[:, 0:2], 0.0, 2.0, ALU.is_ge, ALU.mult).then_inc(sign_step, 1)
                dve.wait_ge(sign_step, 1)
                dve.tensor_scalar(SIGN[:, :], SIGN[:, :], -1.0, None, ALU.add).then_inc(sign_step, 1)
                dve.wait_ge(sign_step, 2)
                dve.tensor_tensor(SIZE[:, 0:2], SCALE[:, 0:2], SIGN[:, :], ALU.mult)
                dve.tensor_scalar(SIGN2[:, 0, :], SIGN[:, :], 2.0, None, ALU.mult)
                dve.tensor_scalar(SIGN2[:, 1, :], SIGN[:, :], -1.0, None, ALU.mult).then_inc(sign_step, 1)
                dve.wait_ge(sign_step, 3)
                dve.tensor_scalar(SIZE[:, 2:3], SIZE[:, 0:1], SIZE[:, 1:2], 8.0, ALU.mult, ALU.mult).then_inc(sign_step, 1)
                dve.wait_ge(sign_step, 4)
                dve.tensor_tensor(SIZE[:, 3:4], SIZE[:, 2:3], SCALE[:, 2:3], ALU.mult).then_inc(sign_step, 1)
                dve.wait_ge(sign_step, 5)
                dve.tensor_scalar(MOD[:, 5, :], MOD[:, 5, :], SIZE[:, 3:4], None, ALU.mult).then_inc(mod_step, 1)

            def turn_q(b):
                wait(dve, q_ready, b.count(1, 1))
                wait(dve, part1, b.count(1, 0))
                dve.tensor_tensor(TURNED[:, 0, :], PA[:, :], ROPE[:, 0, :], ALU.mult).then_inc(turned_q, 1)

            def turn_k(b):
                wait(dve, k_ready, b.count(1, 1))
                dve.tensor_tensor(TURNED[:, 1, :], PA[:, :], ROPE[:, 1, :], ALU.mult).then_inc(turned_k, 1)

            def maximum(b, h):
                wait(dve, s1_ready, b.count(HEADS, h + 1))
                if h == 0:
                    wait(dve, mparts_ready, b.count(1, -1))
                dve.tensor_reduce(NMAX[:, b.pair, :, h % 2, h // 2], S1[s1_bank(h)][:, :, :], AX.X, ALU.max,
                                  negate=True).then_inc(max_ready, 1)

            def split_max(b):
                wait(dve, max_ready, b.count(HEADS, HEADS))
                wait(dve, mT_ready, b.count(1, 0))
                if b.known == 0:
                    dve.wait_ge(ones_set, 1)
                nm = NMAX[:, b.pair]
                part = NPART[:, :, 0:MCOLS].rearrange("p t (a c n) -> p t a c n", a=2, c=PARTS)
                dve.tensor_copy(part[:, :, :, 0, :], nm).then_inc(mpart_step, 1)
                wait(dve, mpart_step, b.count(3, 1))
                dve.tensor_tensor(NREST[:, :, :, :], nm, part[:, :, :, 0, :], ALU.subtract).then_inc(mpart_step, 1)
                wait(dve, mpart_step, b.count(3, 2))
                dve.tensor_copy(part[:, :, :, 1, :], NREST[:, :, :, :]).then_inc(mpart_step, 1)
                wait(dve, mpart_step, b.count(3, 3))
                dve.tensor_tensor(part[:, :, :, 2, :], NREST[:, :, :, :], part[:, :, :, 1, :],
                                  ALU.subtract).then_inc(mparts_ready, 1)

            def normalise_y(b, t):
                wait(dve, y_turned, b.count(2, t + 1))
                if t == 0:
                    wait(dve, yT_ready, b.count(1, 0))
                y = PB[:, :].rearrange("p (h c) -> p h c", c=32)
                dve.reciprocal(RDEN[:, t, :], y[:, :, HEAD_DIM]).then_inc(rden_ready, 1)
                wait(dve, rden_ready, b.count(2, t + 1))
                dve.tensor_tensor(YN[:, t, :].rearrange("p (h d) -> p h d", d=HEAD_DIM), y[:, :, 0:HEAD_DIM],
                                  RDEN[:, t, :].unsqueeze(2).to_broadcast([LANES, HEADS, HEAD_DIM]),
                                  ALU.mult).then_inc(y_normed, 1)

            def add_attention(b):
                wait(dve, o_turned, b.count(1, 1))
                xs = X[:, at(b), :, :] if b.known is not None else X[:, at(b), :, :].rearrange("p o t e -> p (o t) e")
                dve.tensor_tensor(xs, PB[:, 0:SEQ].rearrange("p (t e) -> p t e", t=TILES), xs,
                                  ALU.add).then_inc(x1_ready, 1)

            def iteration(b):
                tail, prep = b.plus(-1), b.plus(3)
                if prep.exists():
                    statistics(prep)
                for h in range(HEADS):
                    m = b.plus(1 + h // LEAD)
                    if prep.exists() and h == 0:
                        wait(dve, bn_ready, prep.count(TILES, TILES))
                    if m.exists():
                        maximum(m, (h + LEAD) % HEADS)
                    if prep.exists() and h == 0:
                        aggregate(prep)
                    if tail.exists():
                        if h == 3:
                            normalise_y(tail, 0)
                        if h == 6:
                            normalise_y(tail, 1)
                        if h == 15:
                            add_attention(tail)
                    if prep.exists():
                        if h == 7:
                            turn_q(prep)
                        if h == 10:
                            turn_k(prep)
                    if b.plus(1).exists() and h == 8:
                        split_max(b.plus(1))
                    if b.known == BATCHES - 1 and h == 5:
                        dve.wait_ge(f_bn, 2)
                        f_aggregate(1)
                    if b.known == BATCHES - 1 and h == 7:
                        h_high(0)
                    if b.known == BATCHES - 1 and h in (9, 10, 12, 14):
                        low(0, 0, (9, 10, 12, 14).index(h))

            def prepare(b):
                turn_q(b)
                turn_k(b)

            def tile_at(g, t, n=1):
                return slice(g * GROUP + t, g * GROUP + t + n) if isinstance(g, int) else bass.ds(g * GROUP + t, n)

            XF = X[:, :, :, :].rearrange("p b t e -> p (b t) e")

            def f_statistics(g):
                if not isinstance(g, int) or g > 0:
                    dve.wait_ge(f_ln, g)
                for t in range(GROUP):
                    ins = dve.bn_stats(FBN[:, t, :], XF[:, tile_at(g, t), :])
                ins.then_inc(f_bn, 1)

            def f_aggregate(g):
                for t in range(GROUP):
                    ins = dve.bn_aggr(FMV[:, t, :], FBN[:, t, :])
                ins.then_inc(f_stats, 1)

            def f_normalise(g):
                dve.wait_ge(f_ln, g + 1)
                if not isinstance(g, int) or g > 0:
                    dve.wait_ge(f_xT, g)
                for t in range(GROUP):
                    ins = dve.tensor_scalar(FXH[:, t:t + 1, :], XF[:, tile_at(g, t), :], FLN[:, 1, t:t + 1],
                                            FLN[:, 3, t:t + 1], ALU.mult, ALU.add)
                ins.then_inc(f_xhat, 1)

            def h_high(g):
                dve.wait_ge(f_hT, g + 1)
                dve.tensor_copy(FHHI[:, :], FH[:, :, :].rearrange("p a t -> p (a t)")).then_inc(f_hhi, 1)

            def low(g, layer, kb):
                dve.wait_ge(hi_ready, g * 8 + (4 * layer + kb + 1))
                dve.scalar_tensor_tensor(LO[layer][:, kb, :], layer_bank(g, layer, kb), 0.0, HI[layer][:, kb, :].bitcast(f32),
                                         ALU.max, ALU.subtract).then_inc(lo_ready, 1)

            def f_output(g):
                dve.wait_ge(y_back, g + 1)
                if not isinstance(g, int) or g > 0:
                    dve.wait_ge(out_stored, g * 16)
                dve.tensor_tensor(OUT[:, :, :], OT[:, :, :].rearrange("p a (t e) -> p (a t) e", e=EMB),
                                  XF[:, tile_at(g, 0, GROUP), :], ALU.add).then_inc(out_ready, 1)

            def f_group(g, ahead):
                if ahead > 0:
                    f_normalise(g + 1)
                low(g, 1, 0)
                f_output(g - 1)
                low(g, 1, 1)
                if ahead > 0:
                    h_high(g + 1)
                if ahead > 1:
                    f_statistics(g + 2)
                    dve.wait_ge(f_bn, g + 3)
                low(g, 1, 2)
                if ahead > 1:
                    f_aggregate(g + 2)
                low(g, 1, 3)
                if ahead > 0:
                    for kb in range(BLOCKS):
                        low(g + 1, 0, kb)

            statistics(Batch(0, 0))
            dve.wait_ge(bn_ready, TILES * 1)
            aggregate(Batch(0, 0))
            modulation()
            statistics(Batch(0, 1))
            dve.wait_ge(bn_ready, TILES * 2)
            aggregate(Batch(0, 1))
            prepare(Batch(0, 0))
            statistics(Batch(0, 2))
            dve.wait_ge(bn_ready, TILES * 3)
            aggregate(Batch(0, 2))
            prepare(Batch(0, 1))
            for h in range(HEADS):
                maximum(Batch(0, 0), h)
            split_max(Batch(0, 0))
            prepare(Batch(0, 2))
            for h in range(LEAD):
                maximum(Batch(0, 1), h)
            for n in range(4):
                dve.wait_ge(x_loaded[n], 16)
            iteration(Batch(0, 0))
            with dve.Fori(0, 3) as turn:
                for j in range(RING):
                    iteration(Batch(turn, 1 + j))
            for b in range(13, BATCHES - 1):
                iteration(Batch(0, b))

            dve.wait_ge(ffn_loaded, 48)
            dve.wait_ge(sign_step, 5)
            dve.tensor_tensor(WDIFF[:, :], U0[:, 0, :], U0[:, 1, :], ALU.subtract).then_inc(wdiff_ready, 1)
            dve.wait_ge(wdiff_ready, 1)
            dve.tensor_scalar(W0[:, :], WDIFF[:, :], SIGN[:, 0:1], None, ALU.mult).then_inc(fw_ready, 1)
            last = Batch(0, BATCHES - 1)
            dve.wait_ge(x1_ready, 4)
            f_statistics(0)
            dve.wait_ge(f_bn, 1)
            f_aggregate(0)
            f_normalise(0)
            f_statistics(1)
            iteration(last)
            f_normalise(1)
            normalise_y(last, 0)
            low(0, 1, 0)
            normalise_y(last, 1)
            h_high(1)
            dve.wait_ge(x1_ready, BATCHES - 1)
            f_statistics(2)
            dve.wait_ge(f_bn, 3)
            low(0, 1, 1)
            f_aggregate(2)
            low(0, 1, 2)
            low(0, 1, 3)
            add_attention(last)
            for kb in range(BLOCKS):
                low(1, 0, kb)
            dve.wait_ge(x1_ready, BATCHES)
            with dve.Fori(1, GROUPS - 2) as g:
                f_group(g, 2)
            f_group(GROUPS - 2, 1)
            f_group(GROUPS - 1, 0)
            f_output(GROUPS - 1)

        @block.tensor
        def _(pe):
            pe.wait_ge(mod_loaded, 48)
            pe.wait_ge(silu_step, 3)
            for j in range(6):
                ins = pe.matmul(PB[:, j * BATCHES:(j + 1) * BATCHES], WMOD[:, j * EMB:(j + 1) * EMB],
                                SILU[:, 0, :], start=True, stop=True)
            ins.then_inc(mod_ready, 1)
            pe.wait_ge(w_loaded, 96)

            def turn_x(b):
                wait(pe, xhat_ready, b.count(1, 1))
                wait(pe, v_copied, b.count(1, 0))
                for t in range(TILES):
                    ins = pe.transpose(PA[:, t * LANES:(t + 1) * LANES], XH[:, t, :], EYE[:, :])
                ins.then_inc(xT_ready, 1)

            def project(b, w, ready, free, free_at):
                wait(pe, free, free_at)
                for s in range(2):
                    ins = pe.matmul(PA[:, s * SEQ:(s + 1) * SEQ], w[:, s, :], HT[:, :], start=True, stop=True)
                ins.then_inc(ready, 1)

            def project_v(b):
                wait(pe, turned_k, b.count(1, 1))
                wait(pe, o_gated, b.count(1, -3))
                for t in range(TILES):
                    ins = pe.matmul(PA[:, t * LANES:(t + 1) * LANES], HT[:, t * LANES:(t + 1) * LANES],
                                    WV[:, :], start=True, stop=True)
                ins.then_inc(v_ready, 1)

            def scores_for_max(b, h):
                base, n = 64 * (h % 2), h // 2
                if h == 0:
                    wait(pe, stack_ready[b.slot], b.in_slot(16 * STACK_DMAS))
                wait(pe, max_ready, b.count(HEADS, s1_bank_read(h)))
                rows = ST[b.slot][base:base + STACK, n, :, :]
                for t in range(TILES):
                    ins = pe.matmul(S1[s1_bank(h)][:, t, :], rows[:, 0, t * LANES:(t + 1) * LANES], rows[:, 1, :],
                                    start=True, stop=True)
                ins.then_inc(s1_ready, 1)

            def turn_max(b):
                wait(pe, mparts_ready, b.count(1, 1))
                wait(pe, y_normed, b.count(2, -2))
                if b.known == 0:
                    pe.wait_ge(mod_step, 1)
                    pe.wait_ge(eyeb_set, 1)
                for t in range(TILES):
                    ins = pe.transpose(MT_PSUM[:, t * LANES:(t + 1) * LANES],
                                       NPART[:, t, :], EYEB[:, :])
                ins.then_inc(mT_ready, 1)

            def shifted_scores(b, h):
                base, n = 64 * (h % 2), h // 2
                if h == 0:
                    wait(pe, mrows_ready[b.slot], b.in_slot(32))
                wait(pe, exp_ready, b.count(HEADS, h - 1))
                rows = ST[b.slot][base:base + SCORE_ROWS, n, :, :]
                for t in range(TILES):
                    ins = pe.matmul(S2[h % 2][:, t, :], rows[:, 1, t * LANES:(t + 1) * LANES], rows[:, 0, :],
                                    start=True, stop=True)
                ins.then_inc(s2_ready, 1)

            def weigh_values(b, quad, t):
                if t == 0:
                    wait(pe, exp_ready, b.count(HEADS, QUAD * quad + QUAD))
                    wait(pe, v_copied, b.count(1, 1))
                    wait(pe, ot_copied, b.count(2, quad // 2))
                for c in range(QUAD):
                    h = QUAD * quad + c
                    ins = pe.matmul(OT[32 * c:32 * c + 32, quad % 2, :], VS[b.slot][:, t, h, :],
                                    PT[:, h % (2 * QUAD), t, :], start=(t == 0), stop=(t == TILES - 1))
                if t == TILES - 1:
                    ins.then_inc(pv_ready, 1)

            def turn_y(b, t):
                if t == 0:
                    wait(pe, ot_copied, b.count(2, 2))
                    wait(pe, x1_ready, b.count(1, 0))
                else:
                    wait(pe, y_normed, b.count(2, 1))
                for q in range(HEADS // QUAD):
                    ins = pe.transpose(PB[:, q * LANES:(q + 1) * LANES], OTS[:, q, t * LANES:(t + 1) * LANES], EYE[:, :])
                ins.then_inc(y_turned, 1)

            def turn_y_back(b):
                wait(pe, y_normed, b.count(2, 2))
                wait(pe, mT_copied, b.capped(3))
                for t in range(TILES):
                    ins = pe.transpose(PB[:, t * LANES:(t + 1) * LANES], YN[:, t, :], EYE[:, :])
                ins.then_inc(yT_ready, 1)

            def project_out(b):
                wait(pe, yT_copied, b.count(1, 1))
                wait(pe, v_copied, b.capped(4))
                wait(pe, turned_k, b.capped(5))
                pe.matmul(PA[:, 0:SEQ], WO[:, :], YT[:, :], start=True, stop=True).then_inc(o_ready, 1)

            def turn_out(b):
                wait(pe, o_gated, b.count(1, 1))
                wait(pe, yT_copied, b.count(1, 1))
                for t in range(TILES):
                    ins = pe.transpose(PB[:, t * LANES:(t + 1) * LANES], OE[:, t * LANES:(t + 1) * LANES], EYE[:, :])
                ins.then_inc(o_turned, 1)

            def iteration(b):
                tail, prep = b.plus(-1), b.plus(3)
                for h in range(HEADS):
                    if b.exists():
                        shifted_scores(b, h)
                    m = b.plus(1 + h // LEAD)
                    if m.exists():
                        scores_for_max(m, (h + LEAD) % HEADS)
                    if tail.exists():
                        if h in (0, 1):
                            weigh_values(tail, 3, h)
                        if h == 3:
                            turn_y(tail, 0)
                        if h == 6:
                            turn_y(tail, 1)
                        if h == 11:
                            turn_y_back(tail)
                        if h == 13:
                            project_out(tail)
                        if h == 15:
                            turn_out(tail)
                    if b.exists() and h in (4, 5, 8, 9, 12, 14):
                        weigh_values(b, (h - 4) // QUAD, int(h not in (4, 8, 12)))
                    if b.plus(2).exists() and h == 2:
                        project_v(b.plus(2))
                    if prep.exists():
                        if h == 5:
                            turn_x(prep)
                        if h == 7:
                            project(prep, WQ, q_ready, hT_ready, prep.count(1, 1))
                        if h == 10:
                            project(prep, WK, k_ready, turned_q, prep.count(1, 1))
                    if b.plus(1).exists() and h == 9:
                        turn_max(b.plus(1))
                    if b.known == BATCHES - 1:
                        if h == 4:
                            pe.wait_ge(v_copied, BATCHES)
                            pe.wait_ge(o_gated, BATCHES - 2)
                            f_turn(0)
                        if h == 8:
                            pe.wait_ge(max_ready, HEADS * BATCHES)
                            pe.wait_ge(fw_ready, 3)
                        if h in (8, 9, 11, 13):
                            f_layer0(0, ((8, 9, 11, 13).index(h),))
                        if h == 12:
                            pe.wait_ge(f_hT, 1)

            def f_turn(g):
                pe.wait_ge(f_xhat, g + 1)
                if not isinstance(g, int) or g > 0:
                    pe.wait_ge(f_hT, g)
                for t in range(GROUP):
                    ins = pe.transpose(PA[:, t * LANES:(t + 1) * LANES], FXH[:, t, :], EYE[:, :])
                ins.then_inc(f_xT, 1)

            def f_layer0(g, blocks=range(BLOCKS)):
                if 0 in blocks:
                    pe.wait_ge(f_hhi, g + 1)
                    pe.wait_ge(f_hlo, g + 1)
                for f in blocks:
                    if isinstance(g, int) and g == 0:
                        if f == 3:
                            pe.wait_ge(lo_ready, 1)
                    elif f > 0:
                        pe.wait_ge(lo_ready, g * 8 + (f - 4))
                    w = W0[:, f * LANES:(f + 1) * LANES]
                    pe.matmul(layer_bank(g, 0, f), w, FHHI[:, :], start=True, stop=False)
                    pe.matmul(layer_bank(g, 0, f), w, FHLO[:, :], start=False, stop=True).then_inc(block_ready, 1)

            def f_layer1(g, f):
                if f == 0:
                    pe.wait_ge(lo_ready, g * 8 + (3 if isinstance(g, int) else 2))
                for kb in range(BLOCKS):
                    if f == 0:
                        pe.wait_ge(lo_ready, g * 8 + (kb + 1))
                    w = W1[:, kb, f * LANES:(f + 1) * LANES]
                    pe.matmul(layer_bank(g, 1, f), w, HI[0][:, kb, :], start=(kb == 0), stop=False)
                    ins = pe.matmul(layer_bank(g, 1, f), w, LO[0][:, kb, :], start=False, stop=(kb == BLOCKS - 1))
                ins.then_inc(block_ready, 1)

            def f_layer2(g):
                if not isinstance(g, int) or g > 0:
                    pe.wait_ge(y_gated, g)
                for kb in range(BLOCKS):
                    pe.wait_ge(lo_ready, g * 8 + (kb + 5))
                    pe.matmul(PB[:, :], W2[:, kb, :], HI[1][:, kb, :], start=(kb == 0), stop=False)
                    ins = pe.matmul(PB[:, :], W2[:, kb, :], LO[1][:, kb, :], start=False, stop=(kb == BLOCKS - 1))
                ins.then_inc(y_ready, 1)

            def f_turn_back(g):
                pe.wait_ge(y_gated, g + 1)
                if not isinstance(g, int) or g > 0:
                    pe.wait_ge(out_ready, g)
                for t in range(GROUP):
                    ins = pe.transpose(OT[:, t // 2, (t % 2) * LANES:(t % 2 + 1) * LANES],
                                       FY[:, t // 2, (t % 2) * LANES:(t % 2 + 1) * LANES], EYE[:, :])
                ins.then_inc(y_back, 1)

            def f_group(g, more):
                f_layer1(g, 0)
                if more:
                    f_turn(g + 1)
                f_turn_back(g - 1)
                f_layer1(g, 1)
                f_layer1(g, 2)
                f_layer1(g, 3)
                if more:
                    f_layer0(g + 1)
                f_layer2(g)


            def prepare(b):
                turn_x(b)
                project(b, WQ, q_ready, hT_ready, b.count(1, 1))
                project(b, WK, k_ready, turned_q, b.count(1, 1))

            prepare(Batch(0, 0))
            project_v(Batch(0, 0))
            prepare(Batch(0, 1))
            project_v(Batch(0, 1))
            for h in range(HEADS):
                scores_for_max(Batch(0, 0), h)
            prepare(Batch(0, 2))
            turn_max(Batch(0, 0))
            for h in range(LEAD):
                scores_for_max(Batch(0, 1), h)
            iteration(Batch(0, 0))
            with pe.Fori(0, 3) as turn:
                for j in range(RING):
                    iteration(Batch(turn, 1 + j))
            for b in range(13, BATCHES - 1):
                iteration(Batch(0, b))

            last = Batch(0, BATCHES - 1)
            iteration(last)
            weigh_values(last, 3, 0)
            weigh_values(last, 3, 1)
            pe.wait_ge(exp_ready, HEADS * BATCHES)
            pe.wait_ge(o_gated, BATCHES - 1)
            f_turn(1)
            turn_y(last, 0)
            f_layer1(0, 0)
            turn_y(last, 1)
            f_layer1(0, 1)
            turn_y_back(last)
            f_layer1(0, 2)
            pe.wait_ge(f_hT, 2)
            project_out(last)
            f_layer1(0, 3)
            turn_out(last)
            f_layer0(1)
            pe.wait_ge(x1_ready, BATCHES)
            f_layer2(0)
            pe.wait_ge(o_gated, BATCHES)
            with pe.Fori(1, GROUPS - 1) as g:
                f_group(g, True)
            f_group(GROUPS - 1, False)
            f_turn_back(GROUPS - 1)


def rope_table():
    i = np.arange(HEAD_DIM // 2, dtype=np.float32)
    rate = np.power(np.float32(10000.0), np.float32(2.0) * i / np.float32(HEAD_DIM))
    theta = np.arange(SEQ, dtype=np.float32)[:, None] * rate[None, :]
    theta = theta.astype(np.float64)
    cos, sin = np.cos(theta), np.sin(theta)
    position = np.arange(SEQ).reshape(LANES, TILES).T.reshape(-1)
    table = np.zeros((LANES, 2, 2, SEQ), np.float64)
    for p in range(LANES):
        d = p % 64 // (HEADS // 2)
        for s, scale in enumerate((1.0 / np.sqrt(HEAD_DIM), 1.0)):
            table[p, s, 0] = cos[position, d // 2] * scale
            table[p, s, 1] = sin[position, d // 2] * scale * (1 if d % 2 else -1)
    return table.reshape(LANES, 2, 2 * SEQ).astype(np.float32)


def kernel(**inputs):
    import concourse.bacc as _bacc
    from concourse.bass_utils import run_bass_kernel_spmd as _run

    a = {k: np.asarray(v) for k, v in inputs.items()}

    def plain_and_swapped(w):
        w = w.reshape(HEADS // 2, 2, HEAD_DIM // 2, 2, EMB)
        both = np.stack([w, w[:, :, :, ::-1]], 0).reshape(2, HEADS // 2, 2, HEAD_DIM, EMB)
        return both.transpose(4, 0, 2, 3, 1).reshape(EMB, 2, EMB)

    arrays = {
        "x": a["L0_attn_x"],
        "wq": plain_and_swapped(a["L0_attn_w_q"]),
        "wk": plain_and_swapped(a["L0_attn_w_k"]),
        "wv": a["L0_attn_w_v"].T,
        "wo": a["L0_attn_w_o"].T,
        "rope": rope_table(),
        "eye": np.eye(LANES, dtype=np.float32),
        "c_t": a["L0_c"].T,
        "wmod": a["L0_wmod"],
        "k0": a["L0_ffn_k0"],
        "k1": a["L0_ffn_k1"],
        "k2": a["L0_ffn_k2"],
        "scales": np.stack([a["L0_ffn_s0"], a["L0_ffn_s1"], a["L0_ffn_s2"]]).reshape(1, 3),
    }
    arrays = {k: np.ascontiguousarray(v) for k, v in arrays.items()}
    nc = _bacc.Bacc("TRN2", target_bir_lowering=False, num_devices=1)
    args = [nc.dram_tensor(f"in_{k}", v.shape, mybir.dt.from_np(v.dtype), kind="ExternalInput").ap()
            for k, v in arrays.items()]
    out = nc.dram_tensor("out", (BATCHES, SEQ, EMB), mybir.dt.float32, kind="ExternalOutput").ap()
    adaln_block(nc, *args, out)
    r = _run(nc, [{f"in_{k}": v for k, v in arrays.items()}], core_ids=[0])
    return r.results[0]["out"]
```

```python
import concourse.bass as bass
from concourse import mybir
from contextlib import ExitStack
import numpy as np

BATCHES, SEQ, EMB, HEADS = 16, 256, 128, 16
HEAD_DIM = EMB // HEADS
HIDDEN = 512
LANES = 128
TILES = SEQ // LANES
PARTS = 3
PRODUCTS = [(0, 0), (0, 1), (0, 2), (1, 0), (1, 1), (2, 0)]
STACK = len(PRODUCTS) * HEAD_DIM
SCORE_ROWS = STACK + PARTS
MCOLS = PARTS * HEADS
RING = 4
QUAD = 4
EPS = 1e-5
TWO_BF16_ONES = float(np.array([0x3F803F80], np.uint32).view(np.float32)[0])
GROUP = 4
GROUPS = BATCHES * TILES // GROUP
BLOCKS = HIDDEN // LANES
LEAD = 7

PE_AT = dict(values=(4, 6, 8, 9, 13, 15), turn_x=7, q=8, k=9, v=11, turn_max=11, turn_y0=3, turn_y1=7, turn_y_back=10, out=15)
ACT_AT = dict(normalise=4, modulate=7, copy_v=13, copy_ot0=9, copy_ot1=1, copy_mt=11, copy_yt=10)
FIRST_AT = dict(turn=2, blocks=(6, 7, 10, 11))
DVE_AT = dict(y0=4, y1=7, q=8, k=9, split=8, add=15)


class Batch:

    def __init__(self, turn, k):
        self.turn, self.k = turn, k
        self.slot, self.pair = k % RING, k % 2
        self.known = k if isinstance(turn, int) else None

    def plus(self, d):
        return Batch(self.turn, self.k + d)

    def exists(self):
        return self.known is None or 0 <= self.known < BATCHES

    def number(self):
        return self.turn * RING + self.k

    def count(self, each, extra):
        return self.turn * (RING * each) + (self.k * each + extra)

    def in_slot(self, each):
        return self.turn * each + (self.k // RING + 1) * each

    def capped(self, ahead):
        n = self.count(1, ahead)
        return min(n, BATCHES) if isinstance(n, int) else n


def wait(engine, sem, value):
    if not isinstance(value, int) or value > 0:
        engine.wait_ge(sem, value)


def adaln_block(nc: bass.Bass, x, wq, wk, wv, wo, rope, eye, c_t, wmod, k0, k1, k2, scales, gate_rows, out):
    f32, f32r, bf16, u8 = mybir.dt.float32, mybir.dt.float32r, mybir.dt.bfloat16, mybir.dt.uint8
    ALU, ACT, AX = mybir.AluOpType, mybir.ActivationFunctionType, mybir.AxisListType
    x_v = x.rearrange("b (p t) e -> p b t e", t=TILES)
    out_v = out.rearrange("b (p t) e -> p b t e", t=TILES)

    ctx = ExitStack()
    with ctx:
        def sb(name, shape, dt=f32):
            return ctx.enter_context(nc.sbuf_tensor(name, shape, dt))

        def ps(name, shape):
            return ctx.enter_context(nc.psum_tensor(name, shape, f32))

        def sem(name):
            return ctx.enter_context(nc.semaphore(name))

        X = sb("X", [LANES, BATCHES, TILES, EMB])
        WQ = sb("WQ", [EMB, 2, EMB])
        WK = sb("WK", [EMB, 2, EMB])
        WV = sb("WV", [EMB, EMB])
        WO = sb("WO", [EMB, EMB])
        ROPE = sb("ROPE", [LANES, 2, 2 * SEQ])
        EYE = sb("EYE", [LANES, LANES])
        EYEB = sb("EYEB", [LANES, LANES], bf16)
        CT = sb("CT", [EMB, BATCHES])
        SILU = sb("SILU", [EMB, 3, BATCHES])
        WMOD = sb("WMOD", [EMB, 6 * EMB])
        MOD = sb("MOD", [EMB, 6, BATCHES])
        GATE = sb("GATE", [EMB, 4, 2, BATCHES])
        SCALE = sb("SCALE", [LANES, 3])
        SIGN = sb("SIGN", [LANES, 2])
        SIGN2 = sb("SIGN2", [LANES, 2, 2])
        SIZE = sb("SIZE", [LANES, 5])
        BN = sb("BN", [LANES, TILES, 6])
        MEANVAR = sb("MEANVAR", [LANES, 2, TILES, 2])
        CONST = sb("CONST", [LANES, 3, GROUP])
        LN = sb("LN", [LANES, 4, TILES])
        XH = sb("XH", [LANES, TILES, EMB])
        HT = sb("HT", [EMB, SEQ])
        TURNED = sb("TURNED", [LANES, 2, 2 * SEQ])
        QK = sb("QK", [LANES, 2, SEQ])
        REST = sb("REST", [LANES, 2, SEQ])
        QKP = [sb(f"QKP{n}", [LANES, 2, PARTS, SEQ], bf16) for n in range(2)]
        ST = [sb(f"ST{r}", [LANES, HEADS // 2, 2, SEQ], bf16) for r in range(RING)]
        VS = [sb(f"VS{r}", [LANES, TILES, HEADS, 32]) for r in range(RING)]
        NMAX = sb("NMAX", [LANES, 2, TILES, 2, HEADS // 2])
        NREST = sb("NREST", [LANES, TILES, 2, HEADS // 2])
        NPART = sb("NPART", [LANES, TILES, LANES], bf16)
        MROW = sb("MROW", [MCOLS, SEQ], bf16)
        PT = sb("PT", [LANES, 2 * QUAD, TILES, SEQ])
        OTS = sb("OTS", [LANES, HEADS // QUAD, SEQ])
        RDEN = sb("RDEN", [LANES, TILES, HEADS])
        YN = sb("YN", [LANES, TILES, EMB])
        YT = sb("YT", [EMB, SEQ])
        GROWS = sb("GROWS", [BATCHES, EMB])
        GA = sb("GA", [LANES, BATCHES, EMB])
        WOG = sb("WOG", [EMB, EMB])
        U0 = sb("U0", [EMB, 2, HIDDEN], u8)
        U1 = sb("U1", [LANES, BLOCKS, HIDDEN], u8)
        U2 = sb("U2", [LANES, BLOCKS, EMB], u8)
        W0 = sb("W0", [EMB, HIDDEN], f32r)
        W1 = sb("W1", [LANES, BLOCKS, HIDDEN], f32r)
        W2 = sb("W2", [LANES, BLOCKS, EMB], f32r)
        FBN = sb("FBN", [LANES, GROUP, 6])
        FMV = sb("FMV", [LANES, GROUP, 2])
        FLN = sb("FLN", [LANES, 4, GROUP])
        FXH = sb("FXH", [LANES, GROUP, EMB])
        FH = sb("FH", [EMB, 2, SEQ])
        WDIFF = sb("WDIFF", [EMB, HIDDEN])
        FHHI = sb("FHHI", [EMB, 2 * SEQ], f32r)
        FHLO = sb("FHLO", [EMB, 2 * SEQ], f32r)
        HI = [sb(f"HI{n}", [LANES, BLOCKS, GROUP * LANES], f32r) for n in range(2)]
        LO = [sb(f"LO{n}", [LANES, BLOCKS, GROUP * LANES], f32r) for n in range(2)]
        FY = sb("FY", [EMB, 2, SEQ])
        OUT = sb("OUT", [LANES, GROUP, EMB])

        S1 = [ps(f"S1{n}", [LANES, TILES, SEQ]) for n in range(3)]
        S2 = [ps(f"S2{n}", [LANES, TILES, SEQ]) for n in range(2)]
        OT = ps("OT", [LANES, 2, SEQ])
        PA = ps("PA", [LANES, 2 * SEQ])
        PB = ps("PB", [LANES, 2 * SEQ])
        MT_PSUM = PB[:, 0:SEQ // 2].bitcast(bf16)
        START = {"q": S2[0], "k": S2[1], "v": OT}
        FBANKS = S1 + S2

        x_loaded = [sem(f"x_loaded{n}") for n in range(5)]
        eye_loaded, wqk_loaded, wv_loaded, wo_loaded = sem("eye_loaded"), sem("wqk_loaded"), sem("wv_loaded"), sem("wo_loaded")
        gates_loaded, rope_loaded = sem("gates_loaded"), sem("rope_loaded")
        mod_loaded = sem("mod_loaded")
        ffn_loaded = sem("ffn_loaded")
        npart_set = sem("npart_set")
        ones_set, row_ones_set, eyeb_set = sem("ones_set"), sem("row_ones_set"), sem("eyeb_set")
        c_exp, silu_step, mod_ready, mod_step = sem("c_exp"), sem("silu_step"), sem("mod_ready"), sem("mod_step")
        bn_ready, stats_ready, ln_step, ln_ready = sem("bn_ready"), sem("stats_ready"), sem("ln_step"), sem("ln_ready")
        xhat_ready, xT_ready, hT_ready = sem("xhat_ready"), sem("xT_ready"), sem("hT_ready")
        q_ready, k_ready, v_ready, v_copied = sem("q_ready"), sem("k_ready"), sem("v_ready"), sem("v_copied")
        turned_q, turned_k, sum_ready = sem("turned_q"), sem("turned_k"), sem("sum_ready")
        part1, rest_ready, part2, part3 = sem("part1"), sem("rest_ready"), sem("part2"), sem("part3")
        stack_ready = [[sem(f"stack_ready_{half}{n}") for n in range(RING)] for half in ("even", "odd")]
        mrows_ready = [[sem(f"mrows_ready_{half}{n}") for n in range(RING)] for half in ("even", "odd")]
        s1_ready, max_ready, mpart_step, mparts_ready = sem("s1_ready"), sem("max_ready"), sem("mpart_step"), sem("mparts_ready")
        mT_ready, mT_copied = sem("mT_ready"), sem("mT_copied")
        s2_ready, exp_ready, pv_ready, ot_copied = sem("s2_ready"), sem("exp_ready"), sem("pv_ready"), sem("ot_copied")
        y_turned, rden_ready, y_normed = sem("y_turned"), sem("rden_ready"), sem("y_normed")
        yT_ready, yT_copied, o_ready, x1_ready = sem("yT_ready"), sem("yT_copied"), sem("o_ready"), sem("x1_ready")
        gates_turned, grows_copied, wog_ready = sem("gates_turned"), sem("grows_copied"), sem("wog_ready")
        grows_stored, ga_loaded = sem("grows_stored"), sem("ga_loaded")
        fw_ready = sem("fw_ready")
        f_bn, f_stats, f_ln_step, f_ln = sem("f_bn"), sem("f_stats"), sem("f_ln_step"), sem("f_ln")
        f_xhat, f_xT, f_hT, f_hhi, f_hlo = sem("f_xhat"), sem("f_xT"), sem("f_hT"), sem("f_hhi"), sem("f_hlo")
        sign_step, wdiff_ready = sem("sign_step"), sem("wdiff_ready")
        block_ready, hi_ready, lo_ready = sem("block_ready"), sem("hi_ready"), sem("lo_ready")
        y_ready, y_gated, y_back, out_ready, out_stored = (sem("y_ready"), sem("y_gated"), sem("y_back"),
                                                           sem("out_ready"), sem("out_stored"))

        STACK_DMAS = len(PRODUCTS)
        FIRST_ORDER = list(range(0, HEADS, 2)) + list(range(1, HEADS, 2))
        X_CHUNKS = [0, 1, 2, 4, 8, 16]

        def s1_bank(h):
            return 1 if h == HEADS - 1 else h % 3

        def s1_bank_read(h):
            before = [g for g in range(h - HEADS, h) if s1_bank(g % HEADS) == s1_bank(h)]
            return before[-1] + 1

        def projection_bank(b, which):
            if b.known in (0, 1, 2):
                return START[which][:, :, :].rearrange("p a t -> p (a t)")
            return PA

        def x_chunk(b):
            return max(n for n in range(5) if X_CHUNKS[n] <= b)

        def layer_bank(g, layer, f):
            if layer == 0:
                f = (1, 2, 0, 1)[f] if isinstance(g, int) and g == 0 else (4, 0, 1, 2)[f]
            return FBANKS[f][:, :, :].rearrange("p a t -> p (a t)")

        block = ctx.enter_context(nc.Block())

        @block.sync
        def _(sp):
            def load_x(n):
                sp.dma_start(X[:, X_CHUNKS[n]:X_CHUNKS[n + 1]], x_v[:, X_CHUNKS[n]:X_CHUNKS[n + 1]]).then_inc(x_loaded[n], 16)

            load_x(0)
            sp.dma_start(CT[:, :], c_t).then_inc(mod_loaded, 16)
            sp.dma_start(WMOD[:, 0:2 * EMB], wmod[:, 0:2 * EMB]).then_inc(mod_loaded, 16)
            sp.dma_start(EYE[:, :], eye).then_inc(eye_loaded, 16)
            for dst, src in ((WQ, wq), (WK, wk)):
                sp.dma_start(dst[:, :, :], src).then_inc(wqk_loaded, 16)
            load_x(1)
            sp.dma_start(ROPE[:, :, :], rope).then_inc(rope_loaded, 16)
            sp.dma_start(WV[:, :], wv).then_inc(wv_loaded, 16)
            sp.dma_start(WMOD[:, 2 * EMB:6 * EMB], wmod[:, 2 * EMB:6 * EMB]).then_inc(gates_loaded, 16)
            sp.dma_start(SCALE[:, :], scales.to_broadcast([LANES, 3])).then_inc(gates_loaded, 16)
            load_x(2)
            sp.dma_start(WO[:, :], wo).then_inc(wo_loaded, 16)
            load_x(3)
            load_x(4)
            sp.dma_start(U0[:, :, :], k0.rearrange("(s p) n -> p s n", s=2)).then_inc(ffn_loaded, 16)
            sp.dma_start(U1[:, :, :], k1.rearrange("(s p) n -> p s n", s=BLOCKS)).then_inc(ffn_loaded, 16)
            sp.dma_start(U2[:, :, :], k2.rearrange("(s p) n -> p s n", s=BLOCKS)).then_inc(ffn_loaded, 16)

            def stack(b, parts, last, halves=(0, 1)):
                wait(sp, parts, b.count(1, 1))
                if b.known is not None and b.known < RING and last == 0:
                    sp.wait_ge(row_ones_set, b.known + 1)
                for j, (qp, kp) in enumerate(PRODUCTS):
                    for half in halves if max(qp, kp) == last else ():
                        row, src = 64 * half + HEAD_DIM * j, QKP[b.pair][64 * half:64 * half + 64, :, :, :]
                        src = src.rearrange("p a c t -> p (a c) t")[:, qp:PARTS + kp + 1:PARTS + kp - qp, :]
                        sp.dma_start(ST[b.slot][row:row + HEAD_DIM, :, :, :], src).then_inc(stack_ready[half][b.slot], 16)

            def max_rows(b):
                wait(sp, mT_copied, b.count(1, 1))
                for half in range(2):
                    row, n = 64 * half + STACK, PARTS * HEADS // 2
                    sp.dma_start(ST[b.slot][row:row + PARTS, :, 0, :],
                                 MROW[half * n:(half + 1) * n, :]).then_inc(mrows_ready[half][b.slot], 16)

            def whole_stack(b):
                for last, parts in enumerate((part1, part2, part3)):
                    stack(b, parts, last)

            def iteration(b):
                if b.plus(1).exists():
                    max_rows(b.plus(1))
                if b.plus(3).exists():
                    whole_stack(b.plus(3))

            for half in range(2):
                for last, parts in enumerate((part1, part2, part3)):
                    stack(Batch(0, 0), parts, last, (half,))
            sp.wait_ge(grows_copied, 1)
            sp.dma_start(gate_rows, GROWS[:, :]).then_inc(grows_stored, 16)
            whole_stack(Batch(0, 1))
            sp.wait_ge(grows_stored, 16)
            sp.dma_start(GA[:, :, :].rearrange("p b e -> p (b e)"),
                         gate_rows.rearrange("b e -> (b e)").unsqueeze(0).to_broadcast([LANES, BATCHES * EMB])).then_inc(ga_loaded, 16)
            stack(Batch(0, 2), part1, 0)
            stack(Batch(0, 2), part2, 1)
            max_rows(Batch(0, 0))
            stack(Batch(0, 2), part3, 2)
            iteration(Batch(0, 0))
            with sp.Fori(0, 3) as turn:
                for j in range(RING):
                    iteration(Batch(turn, 1 + j))
            for b in range(13, BATCHES):
                iteration(Batch(0, b))

            for g in range(GROUPS):
                sp.wait_ge(out_ready, g + 1)
                sp.dma_start(out_v[:, 2 * g:2 * g + 2, :, :], OUT[:, :, :]).then_inc(out_stored, 16)
            sp.wait_ge(out_stored, 16 * GROUPS)

        @block.gpsimd
        def _(pool):
            for n, value in enumerate((-0.5, EPS, -1.0)):
                pool.memset(CONST[:, n, :], value)
            def constants(r):
                pool.memset(VS[r][:, :, :, HEAD_DIM + 1:32], 0.0)
                pool.memset(VS[r][:, :, :, HEAD_DIM:HEAD_DIM + 1], 1.0).then_inc(ones_set, 1)

            def layer_norm(b):
                wait(pool, stats_ready, b.count(1, 1))
                wait(pool, xhat_ready, b.count(1, 0))
                mv = MEANVAR[:, b.pair]
                pool.tensor_tensor(LN[:, 0, :], mv[:, :, 1], CONST[:, 1, 0:TILES], ALU.add).then_inc(ln_step, 1)
                pool.tensor_tensor(LN[:, 2, :], mv[:, :, 0], CONST[:, 2, 0:TILES], ALU.mult).then_inc(ln_step, 1)
                wait(pool, ln_step, b.count(3, 1))
                pool.tensor_tensor(LN[:, 1, :], LN[:, 0, :], CONST[:, 0, 0:TILES], ALU.pow).then_inc(ln_step, 1)
                wait(pool, ln_step, b.count(3, 3))
                pool.tensor_tensor(LN[:, 3, :], LN[:, 2, :], LN[:, 1, :], ALU.mult).then_inc(ln_ready, 1)

            def rotate_and_split(b):
                wait(pool, turned_k, b.count(1, 1))
                wait(pool, part3, b.count(1, 0))
                pool.tensor_tensor(QK[:, :, :], TURNED[:, :, 0:SEQ], TURNED[:, :, SEQ:2 * SEQ],
                                   ALU.add).then_inc(sum_ready, 1)
                first_part(b)
                wait(pool, sum_ready, b.count(1, 1))
                wait(pool, part1, b.count(1, 1))
                second_part(b)
                pool.tensor_tensor(REST[:, :, :], QK[:, :, :], QKP[b.pair][:, :, 0, :], ALU.subtract).then_inc(rest_ready, 1)
                wait(pool, rest_ready, b.count(1, 1))
                wait(pool, part2, b.count(1, 1))
                pool.tensor_tensor(QKP[b.pair][:, :, 2, :], REST[:, :, :], QKP[b.pair][:, :, 1, :],
                                   ALU.subtract).then_inc(part3, 1)

            def first_part(b):
                if b.k > 1 or b.known is None:
                    before = b.plus(-2)
                    for half in range(2):
                        wait(pool, stack_ready[half][before.slot], before.in_slot(16 * STACK_DMAS))
                wait(pool, s2_ready, b.count(HEADS, -(RING - 1) * HEADS))
                pool.tensor_tensor(QKP[b.pair][:, :, 0, :], TURNED[:, :, 0:SEQ], TURNED[:, :, SEQ:2 * SEQ],
                                   ALU.add).then_inc(part1, 1)

            def second_part(b):
                pool.tensor_tensor(QKP[b.pair][:, :, 1, :], QK[:, :, :], QKP[b.pair][:, :, 0, :],
                                   ALU.subtract).then_inc(part2, 1)

            def gate_weights(b):
                wait(pool, o_ready, b.count(1, 0))
                ga = GA[:, b.known, :] if b.known is not None else GA[:, bass.ds(b.number(), 1), :].rearrange("p o e -> p (o e)")
                pool.tensor_tensor(WOG[:, :], WO[:, :], ga, ALU.mult).then_inc(wog_ready, 1)

            def iteration(b):
                if b.plus(3).exists():
                    layer_norm(b.plus(3))
                if b.plus(-1).exists():
                    gate_weights(b.plus(-1))
                if b.plus(3).exists():
                    rotate_and_split(b.plus(3))

            def row_ones(r):
                pool.memset(ST[r][:, :, 1, :].bitcast(f32), TWO_BF16_ONES).then_inc(row_ones_set, 1)

            row_ones(0)
            pool.wait_ge(row_ones_set, 1)
            layer_norm(Batch(0, 0))
            row_ones(1)
            layer_norm(Batch(0, 1))
            constants(0)
            pool.memset(NPART[:, :, :], 0.0).then_inc(npart_set, 1)
            constants(1)
            for n in range(2):
                pool.wait_ge(turned_k, n + 1)
                first_part(Batch(0, n))
                pool.wait_ge(sum_ready, n + 1)
                pool.wait_ge(part1, n + 1)
                second_part(Batch(0, n))
                if n == 0:
                    layer_norm(Batch(0, 2))
                    row_ones(2)
                    constants(2)
            rotate_and_split(Batch(0, 2))
            row_ones(3)
            constants(3)
            iteration(Batch(0, 0))
            pool.wait_ge(wo_loaded, 16)
            pool.wait_ge(ga_loaded, 16)
            with pool.Fori(0, 3) as turn:
                for j in range(RING):
                    iteration(Batch(turn, 1 + j))

            pool.wait_ge(ffn_loaded, 48)
            pool.wait_ge(sign_step, 5)
            pool.tensor_scalar(W1[:, :, :], U1[:, :, :], SIGN2[:, 0, 1:2], SIGN2[:, 1, 1:2],
                               ALU.mult, ALU.add).then_inc(fw_ready, 1)
            pool.tensor_scalar(W2[:, :, :], U2[:, :, :], 2.0, -1.0, ALU.mult, ALU.add).then_inc(fw_ready, 1)

            def f_norm(g):
                pool.wait_ge(f_stats, g + 1)
                if not isinstance(g, int) or g > 0:
                    pool.wait_ge(f_xhat, g)
                pool.tensor_tensor(FLN[:, 0, :], FMV[:, :, 1], CONST[:, 1, :], ALU.add).then_inc(f_ln_step, 1)
                pool.wait_ge(f_ln_step, g * 3 + 1)
                pool.tensor_tensor(FLN[:, 1, :], FLN[:, 0, :], CONST[:, 0, :], ALU.pow).then_inc(f_ln_step, 1)
                pool.wait_ge(f_ln_step, g * 3 + 2)
                pool.tensor_tensor(FLN[:, 2, :], FMV[:, :, 0], FLN[:, 1, :], ALU.mult).then_inc(f_ln_step, 1)
                pool.wait_ge(f_ln_step, g * 3 + 3)
                pool.tensor_tensor(FLN[:, 3, :], FLN[:, 2, :], CONST[:, 2, :], ALU.mult).then_inc(f_ln, 1)

            def h_low(g):
                pool.wait_ge(f_hhi, g + 1)
                pool.tensor_tensor(FHLO[:, :], FH[:, :, :].rearrange("p a t -> p (a t)"),
                                   FHHI[:, :].bitcast(f32), ALU.subtract).then_inc(f_hlo, 1)

            gate_weights(Batch(0, 12))
            gate_weights(Batch(0, 13))
            f_norm(0)
            gate_weights(Batch(0, 14))
            h_low(0)
            f_norm(1)
            gate_weights(Batch(0, 15))
            h_low(1)
            with pool.Fori(2, GROUPS) as g:
                f_norm(g)
                h_low(g)

        @block.scalar
        def _(act):
            act.wait_ge(mod_loaded, 32)
            act.activation(SILU[:, 0, :], CT[:, :], ACT.Exp, scale=-1.0).then_inc(c_exp, 1)

            def normalise(b):
                wait(act, ln_ready, b.count(1, 1))
                wait(act, xT_ready, b.count(1, 0))
                for t in range(TILES):
                    ins = act.activation(XH[:, t, :], X[:, at(b), t, :], ACT.Identity,
                                         bias=LN[:, 3, t:t + 1], scale=LN[:, 1, t:t + 1])
                ins.then_inc(xhat_ready, 1)

            def at(b):
                return b.known if b.known is not None else bass.ds(b.number(), 1)

            def col(tile, j, b):
                n = b.number() if b.known is None else b.known
                return tile[:, j, bass.ds(n, 1)] if b.known is None else tile[:, j, n:n + 1]

            def modulate(b):
                wait(act, xT_ready, b.count(1, 1))
                if b.known == 0:
                    act.wait_ge(mod_step, 2)
                act.activation(HT[:, :], PA[:, 0:SEQ], ACT.Identity, bias=col(MOD, 0, b),
                               scale=col(MOD, 1, b)).then_inc(hT_ready, 1)

            def copy_v(b):
                wait(act, v_ready, b.count(1, 1))
                wait(act, pv_ready, b.count(4, -4 * (RING - 1)))
                if b.known is not None and b.known < RING:
                    act.wait_ge(ones_set, b.known + 1)
                act.activation(VS[b.slot][:, :, :, 0:HEAD_DIM],
                               projection_bank(b, "v")[:, 0:SEQ].rearrange("p (t h d) -> p t h d", t=TILES, h=HEADS),
                               ACT.Copy).then_inc(v_copied, 1)

            def exps(b, h):
                wait(act, s2_ready, b.count(HEADS, h + 1))
                if h % QUAD == 0:
                    wait(act, pv_ready, b.count(4, h // QUAD - 1))
                act.activation(PT[:, h % (2 * QUAD), :, :], S2[h % 2][:, :, :], ACT.Exp).then_inc(exp_ready, 1)

            def copy_ot(b, half):
                wait(act, pv_ready, b.count(4, 2 * half + 2))
                wait(act, y_turned, b.count(2, 0))
                act.activation(OTS[:, 2 * half:2 * half + 2, :], OT[:, :, :],
                               ACT.Copy).then_inc(ot_copied, 1)

            def copy_yt(b):
                wait(act, yT_ready, b.count(1, 1))
                wait(act, o_ready, b.count(1, 0))
                act.activation(YT[:, :], PB[:, 0:SEQ], ACT.Copy).then_inc(yT_copied, 1)

            def copy_mt(b):
                wait(act, mT_ready, b.count(1, 1))
                if b.k > 0 or b.known is None:
                    before = b.plus(-1)
                    for half in range(2):
                        wait(act, mrows_ready[half][before.slot], before.in_slot(16))
                act.activation(MROW[:, :], MT_PSUM[0:MCOLS, :], ACT.Copy).then_inc(mT_copied, 1)

            def iteration(b):
                tail, prep = b.plus(-1), b.plus(3)
                for h in range(HEADS):
                    if b.exists():
                        exps(b, h)
                    if tail.exists():
                        if h == ACT_AT["copy_ot1"]:
                            copy_ot(tail, 1)
                        if h == ACT_AT["copy_yt"]:
                            copy_yt(tail)
                    if prep.exists():
                        if h == ACT_AT["normalise"]:
                            normalise(prep)
                        if h == ACT_AT["modulate"]:
                            modulate(prep)
                        if h == ACT_AT["copy_v"]:
                            copy_v(prep)
                    if b.exists() and h == ACT_AT["copy_ot0"]:
                        copy_ot(b, 0)
                    if b.known == BATCHES - 1 and h == FIRST_AT["turn"]:
                        f_mod(0)
                    if b.plus(1).exists() and h == ACT_AT["copy_mt"]:
                        copy_mt(b.plus(1))

            normalise(Batch(0, 0))
            for n in range(3):
                modulate(Batch(0, n))
                if n < 2:
                    normalise(Batch(0, n + 1))
                else:
                    act.wait_ge(gates_turned, 1)
                    act.activation(GROWS[:, :], PB[0:BATCHES, 0:EMB], ACT.Copy).then_inc(grows_copied, 1)
                copy_v(Batch(0, n))
            copy_mt(Batch(0, 0))
            iteration(Batch(0, 0))
            with act.Fori(0, 3) as turn:
                for j in range(RING):
                    iteration(Batch(turn, 1 + j))
            for b in range(13, BATCHES - 1):
                iteration(Batch(0, b))

            def f_mod(g):
                act.wait_ge(f_xT, g + 1)
                if not isinstance(g, int) or g > 0:
                    act.wait_ge(f_hlo, g)
                for u in range(2):
                    n = g * 2 + u
                    c = slice(n, n + 1) if isinstance(g, int) else bass.ds(n, 1)
                    ins = act.activation(FH[:, u, :], PA[:, u * SEQ:(u + 1) * SEQ], ACT.Identity,
                                         bias=MOD[:, 3, c], scale=MOD[:, 4, c])
                ins.then_inc(f_hT, 1)

            def f_relu(g, layer, kb):
                act.wait_ge(block_ready, g * 8 + (4 * layer + kb + 1))
                act.activation(HI[layer][:, kb, :], layer_bank(g, layer, kb), ACT.Relu).then_inc(hi_ready, 1)

            def f_gate(g):
                act.wait_ge(y_ready, g + 1)
                if not isinstance(g, int) or g > 0:
                    act.wait_ge(y_back, g)
                for u in range(2):
                    n = g * 2 + u
                    c = slice(n, n + 1) if isinstance(g, int) else bass.ds(n, 1)
                    ins = act.activation(FY[:, u, :], PB[:, u * SEQ:(u + 1) * SEQ], ACT.Identity,
                                         scale=MOD[:, 5, c])
                ins.then_inc(y_gated, 1)

            def f_group(g, more):
                f_relu(g, 1, 0)
                if more:
                    f_mod(g + 1)
                f_relu(g, 1, 1)
                f_relu(g, 1, 2)
                f_relu(g, 1, 3)
                if more:
                    for kb in range(BLOCKS):
                        f_relu(g + 1, 0, kb)
                f_gate(g)

            last = Batch(0, BATCHES - 1)
            iteration(last)
            copy_ot(last, 1)
            f_mod(1)
            f_relu(0, 1, 0)
            f_relu(0, 1, 1)
            copy_yt(last)
            f_relu(0, 1, 2)
            f_relu(0, 1, 3)
            for kb in range(BLOCKS):
                f_relu(1, 0, kb)
            f_gate(0)
            with act.Fori(1, GROUPS - 1) as g:
                f_group(g, True)
            f_group(GROUPS - 1, False)

        @block.vector
        def _(dve):
            def at(b):
                return b.known if b.known is not None else bass.ds(b.number(), 1)

            def statistics(b):
                if b.known is not None and b.known < 4:
                    dve.wait_ge(x_loaded[x_chunk(b.known)], 16)
                wait(dve, stats_ready, b.count(1, 0))
                wait(dve, ln_ready, b.count(1, -1))
                for t in range(TILES):
                    dve.bn_stats(BN[:, t, :], X[:, at(b), t, :]).then_inc(bn_ready, 1)

            def aggregate(b):
                for t in range(TILES):
                    ins = dve.bn_aggr(MEANVAR[:, b.pair, t, :], BN[:, t, :])
                ins.then_inc(stats_ready, 1)

            def modulation_first():
                dve.wait_ge(mod_ready, 1)
                dve.tensor_copy(MOD[:, 0, :], PB[:, 0:BATCHES]).then_inc(mod_step, 1)
                dve.tensor_scalar(MOD[:, 1, :], PB[:, BATCHES:2 * BATCHES], 1.0, None, ALU.add).then_inc(mod_step, 1)

            def modulation():
                dve.wait_ge(mod_ready, 2)
                dve.tensor_copy(MOD[:, 2:6, :], PB[:, 2 * BATCHES:6 * BATCHES].rearrange("p (j b) -> p j b", j=4)).then_inc(mod_step, 1)
                dve.wait_ge(mod_step, 3)
                dve.tensor_scalar(MOD[:, 4, :], MOD[:, 4, :], 1.0, None, ALU.add)
                dve.tensor_scalar(GATE[:, 0], MOD[:, 2:6:3, :], -1.0, None, ALU.mult)
                dve.tensor_scalar(GATE[:, 1], MOD[:, 2:6:3, :], 0.0, 2.0, ALU.is_ge, ALU.mult).then_inc(mod_step, 1)
                dve.wait_ge(mod_step, 4)
                dve.tensor_tensor(GATE[:, 2], MOD[:, 2:6:3, :], GATE[:, 0], ALU.max).then_inc(mod_step, 1)
                dve.wait_ge(mod_step, 5)
                dve.tensor_scalar(GATE[:, 3], GATE[:, 2], 0.25, None, ALU.max)
                dve.tensor_scalar(GATE[:, 0], GATE[:, 1], -1.0, None, ALU.add).then_inc(mod_step, 1)
                dve.wait_ge(mod_step, 6)
                dve.tensor_tensor(MOD[:, 2:6:3, :], GATE[:, 0], GATE[:, 3], ALU.mult).then_inc(mod_step, 1)
                dve.wait_ge(mod_step, 7)
                dve.tensor_scalar(SIGN[:, :], SCALE[:, 0:2], 0.0, 2.0, ALU.is_ge, ALU.mult).then_inc(sign_step, 1)
                dve.wait_ge(sign_step, 1)
                dve.tensor_scalar(SIGN[:, :], SIGN[:, :], -1.0, None, ALU.add).then_inc(sign_step, 1)
                dve.wait_ge(sign_step, 2)
                dve.tensor_tensor(SIZE[:, 0:2], SCALE[:, 0:2], SIGN[:, :], ALU.mult)
                dve.tensor_scalar(SIGN2[:, 0, :], SIGN[:, :], 2.0, None, ALU.mult)
                dve.tensor_scalar(SIGN2[:, 1, :], SIGN[:, :], -1.0, None, ALU.mult).then_inc(sign_step, 1)
                dve.wait_ge(sign_step, 3)
                dve.tensor_scalar(SIZE[:, 2:3], SIZE[:, 0:1], SIZE[:, 1:2], 8.0, ALU.mult, ALU.mult).then_inc(sign_step, 1)
                dve.wait_ge(sign_step, 4)
                dve.tensor_tensor(SIZE[:, 3:4], SIZE[:, 2:3], SCALE[:, 2:3], ALU.mult).then_inc(sign_step, 1)
                dve.wait_ge(sign_step, 5)
                dve.tensor_scalar(MOD[:, 5, :], MOD[:, 5, :], SIZE[:, 3:4], None, ALU.mult).then_inc(mod_step, 1)

            def turn_q(b):
                wait(dve, q_ready, b.count(1, 1))
                wait(dve, part1, b.count(1, 0))
                if b.known in (1, 2):
                    dve.wait_ge(sum_ready, b.known)
                dve.tensor_tensor(TURNED[:, 0, :], projection_bank(b, "q")[:, :], ROPE[:, 0, :], ALU.mult).then_inc(turned_q, 1)

            def turn_k(b):
                wait(dve, k_ready, b.count(1, 1))
                dve.tensor_tensor(TURNED[:, 1, :], projection_bank(b, "k")[:, :], ROPE[:, 1, :], ALU.mult).then_inc(turned_k, 1)

            def maximum(b, h, at=None):
                at = h if at is None else at
                wait(dve, s1_ready, b.count(HEADS, at + 1))
                if at == 0:
                    wait(dve, mparts_ready, b.count(1, -1))
                dve.tensor_reduce(NMAX[:, b.pair, :, h % 2, h // 2], S1[s1_bank(at)][:, :, :], AX.X, ALU.max,
                                  negate=True).then_inc(max_ready, 1)

            def split_max(b):
                wait(dve, max_ready, b.count(HEADS, HEADS))
                wait(dve, mT_ready, b.count(1, 0))
                if b.known == 0:
                    dve.wait_ge(npart_set, 1)
                nm = NMAX[:, b.pair]
                part = NPART[:, :, 0:MCOLS].rearrange("p t (a c n) -> p t a c n", a=2, c=PARTS)
                dve.tensor_copy(part[:, :, :, 0, :], nm).then_inc(mpart_step, 1)
                wait(dve, mpart_step, b.count(3, 1))
                dve.tensor_tensor(NREST[:, :, :, :], nm, part[:, :, :, 0, :], ALU.subtract).then_inc(mpart_step, 1)
                wait(dve, mpart_step, b.count(3, 2))
                dve.tensor_copy(part[:, :, :, 1, :], NREST[:, :, :, :]).then_inc(mpart_step, 1)
                wait(dve, mpart_step, b.count(3, 3))
                dve.tensor_tensor(part[:, :, :, 2, :], NREST[:, :, :, :], part[:, :, :, 1, :],
                                  ALU.subtract).then_inc(mparts_ready, 1)

            def normalise_y(b, t):
                wait(dve, y_turned, b.count(2, t + 1))
                if t == 0:
                    wait(dve, yT_ready, b.count(1, 0))
                y = PB[:, :].rearrange("p (h c) -> p h c", c=32)
                dve.reciprocal(RDEN[:, t, :], y[:, :, HEAD_DIM]).then_inc(rden_ready, 1)
                wait(dve, rden_ready, b.count(2, t + 1))
                dve.tensor_tensor(YN[:, t, :].rearrange("p (h d) -> p h d", d=HEAD_DIM), y[:, :, 0:HEAD_DIM],
                                  RDEN[:, t, :].unsqueeze(2).to_broadcast([LANES, HEADS, HEAD_DIM]),
                                  ALU.mult).then_inc(y_normed, 1)

            def add_attention(b):
                wait(dve, o_ready, b.count(1, 1))
                xs = X[:, at(b), :, :] if b.known is not None else X[:, at(b), :, :].rearrange("p o t e -> p (o t) e")
                dve.tensor_tensor(xs, PA[:, 0:SEQ].rearrange("p (t e) -> p t e", t=TILES), xs,
                                  ALU.add).then_inc(x1_ready, 1)

            def iteration(b):
                tail, prep = b.plus(-1), b.plus(3)
                if prep.exists():
                    statistics(prep)
                for h in range(HEADS):
                    m = b.plus(1 + (h + LEAD) // HEADS)
                    if prep.exists() and h == 0:
                        wait(dve, bn_ready, prep.count(TILES, TILES))
                    if m.exists():
                        maximum(m, (h + LEAD) % HEADS)
                    if prep.exists() and h == 0:
                        aggregate(prep)
                    if tail.exists():
                        if h == DVE_AT["y0"]:
                            normalise_y(tail, 0)
                        if h == DVE_AT["y1"]:
                            normalise_y(tail, 1)
                        if h == DVE_AT["add"]:
                            add_attention(tail)
                    if prep.exists():
                        if h == DVE_AT["q"]:
                            turn_q(prep)
                        if h == DVE_AT["k"]:
                            turn_k(prep)
                    if b.plus(1).exists() and h == DVE_AT["split"]:
                        split_max(b.plus(1))
                    if b.known == BATCHES - 3 and h == 6:
                        weights()
                    if b.known == BATCHES - 2:
                        if h == 2:
                            dve.wait_ge(x1_ready, 4)
                            f_statistics(0)
                        if h == 4:
                            dve.wait_ge(f_bn, 1)
                            f_aggregate(0)
                        if h == 10:
                            f_normalise(0)
                        if h == 12:
                            f_statistics(1)
                        if h == 13:
                            dve.wait_ge(f_bn, 2)
                            f_aggregate(1)
                    if b.known == BATCHES - 1 and h == FIRST_AT["turn"]:
                        h_high(0)
                    if b.known == BATCHES - 1 and h in FIRST_AT["blocks"]:
                        high(0, 0, FIRST_AT["blocks"].index(h))
                        low(0, 0, FIRST_AT["blocks"].index(h))

            def tile_at(g, t, n=1):
                return slice(g * GROUP + t, g * GROUP + t + n) if isinstance(g, int) else bass.ds(g * GROUP + t, n)

            XF = X[:, :, :, :].rearrange("p b t e -> p (b t) e")

            def f_statistics(g):
                if not isinstance(g, int) or g > 0:
                    dve.wait_ge(f_ln, g)
                for t in range(GROUP):
                    ins = dve.bn_stats(FBN[:, t, :], XF[:, tile_at(g, t), :])
                ins.then_inc(f_bn, 1)

            def f_aggregate(g):
                for t in range(GROUP):
                    ins = dve.bn_aggr(FMV[:, t, :], FBN[:, t, :])
                ins.then_inc(f_stats, 1)

            def f_normalise(g):
                dve.wait_ge(f_ln, g + 1)
                if not isinstance(g, int) or g > 0:
                    dve.wait_ge(f_xT, g)
                for t in range(GROUP):
                    ins = dve.tensor_scalar(FXH[:, t:t + 1, :], XF[:, tile_at(g, t), :], FLN[:, 1, t:t + 1],
                                            FLN[:, 3, t:t + 1], ALU.mult, ALU.add)
                ins.then_inc(f_xhat, 1)

            def h_high(g):
                dve.wait_ge(f_hT, g + 1)
                dve.tensor_copy(FHHI[:, :], FH[:, :, :].rearrange("p a t -> p (a t)")).then_inc(f_hhi, 1)

            def weights():
                dve.wait_ge(ffn_loaded, 48)
                dve.wait_ge(sign_step, 5)
                dve.tensor_tensor(WDIFF[:, :], U0[:, 0, :], U0[:, 1, :], ALU.subtract).then_inc(wdiff_ready, 1)
                dve.wait_ge(wdiff_ready, 1)
                dve.tensor_scalar(W0[:, :], WDIFF[:, :], SIGN[:, 0:1], None, ALU.mult).then_inc(fw_ready, 1)

            def high(g, layer, kb):
                dve.wait_ge(block_ready, g * 8 + (4 * layer + kb + 1))
                dve.tensor_scalar(HI[layer][:, kb, :], layer_bank(g, layer, kb), 0.0, None, ALU.max).then_inc(hi_ready, 1)

            def low(g, layer, kb):
                dve.wait_ge(hi_ready, g * 8 + (4 * layer + kb + 1))
                dve.scalar_tensor_tensor(LO[layer][:, kb, :], layer_bank(g, layer, kb), 0.0, HI[layer][:, kb, :].bitcast(f32),
                                         ALU.max, ALU.subtract).then_inc(lo_ready, 1)

            def f_output(g):
                dve.wait_ge(y_back, g + 1)
                if not isinstance(g, int) or g > 0:
                    dve.wait_ge(out_stored, g * 16)
                dve.tensor_tensor(OUT[:, :, :], OT[:, :, :].rearrange("p a (t e) -> p (a t) e", e=EMB),
                                  XF[:, tile_at(g, 0, GROUP), :], ALU.add).then_inc(out_ready, 1)

            def f_group(g, ahead):
                if ahead > 0:
                    f_normalise(g + 1)
                low(g, 1, 0)
                f_output(g - 1)
                low(g, 1, 1)
                if ahead > 0:
                    h_high(g + 1)
                if ahead > 1:
                    f_statistics(g + 2)
                    dve.wait_ge(f_bn, g + 3)
                low(g, 1, 2)
                if ahead > 1:
                    f_aggregate(g + 2)
                low(g, 1, 3)
                if ahead > 0:
                    for kb in range(BLOCKS):
                        low(g + 1, 0, kb)

            def sum_parts(b):
                wait(dve, turned_k, b.count(1, 1))
                wait(dve, part2, b.count(1, 0))
                dve.tensor_tensor(QK[:, :, :], TURNED[:, :, 0:SEQ], TURNED[:, :, SEQ:2 * SEQ],
                                  ALU.add).then_inc(sum_ready, 1)

            def rest_part(b):
                wait(dve, sum_ready, b.count(1, 1))
                wait(dve, part1, b.count(1, 1))
                wait(dve, part3, b.count(1, 0))
                dve.tensor_tensor(REST[:, :, :], QK[:, :, :], QKP[b.pair][:, :, 0, :], ALU.subtract).then_inc(rest_ready, 1)

            def third_part(b):
                wait(dve, rest_ready, b.count(1, 1))
                wait(dve, part2, b.count(1, 1))
                dve.tensor_tensor(QKP[b.pair][:, :, 2, :], REST[:, :, :], QKP[b.pair][:, :, 1, :],
                                  ALU.subtract).then_inc(part3, 1)

            def measure(b):
                statistics(b)
                dve.wait_ge(bn_ready, TILES * (b.known + 1))
                aggregate(b)

            first, second, third = (Batch(0, n) for n in range(3))
            measure(first)
            dve.wait_ge(c_exp, 1)
            dve.tensor_scalar(SILU[:, 1, :], SILU[:, 0, :], 1.0, None, ALU.add).then_inc(silu_step, 1)
            dve.wait_ge(silu_step, 1)
            dve.reciprocal(SILU[:, 2, :], SILU[:, 1, :]).then_inc(silu_step, 1)
            dve.wait_ge(silu_step, 2)
            dve.tensor_tensor(SILU[:, 0, :], SILU[:, 2, :], CT[:, :], ALU.mult).then_inc(silu_step, 1)
            modulation_first()
            measure(second)
            dve.wait_ge(rope_loaded, 16)
            turn_q(first)
            turn_k(first)
            sum_parts(first)
            rest_part(first)
            third_part(first)
            measure(third)
            modulation()
            turn_q(second)
            turn_k(second)
            dve.wait_ge(eye_loaded, 16)
            dve.tensor_copy(EYEB[:, :], EYE[:, :]).then_inc(eyeb_set, 1)
            sum_parts(second)
            for n, h in enumerate(FIRST_ORDER):
                if n == 1:
                    rest_part(second)
                if n == 3:
                    third_part(second)
                if n == 4:
                    turn_q(third)
                if n == 6:
                    turn_k(third)
                maximum(Batch(0, 0), h, n)
            split_max(Batch(0, 0))
            for h in range(LEAD):
                maximum(Batch(0, 1), h)
            for n in range(5):
                dve.wait_ge(x_loaded[n], 16)
            iteration(Batch(0, 0))
            with dve.Fori(0, 3) as turn:
                for j in range(RING):
                    iteration(Batch(turn, 1 + j))
            for b in range(13, BATCHES - 1):
                iteration(Batch(0, b))
            last = Batch(0, BATCHES - 1)
            iteration(last)
            f_normalise(1)
            normalise_y(last, 0)
            low(0, 1, 0)
            normalise_y(last, 1)
            h_high(1)
            dve.wait_ge(x1_ready, BATCHES - 1)
            f_statistics(2)
            dve.wait_ge(f_bn, 3)
            low(0, 1, 1)
            f_aggregate(2)
            low(0, 1, 2)
            low(0, 1, 3)
            add_attention(last)
            for kb in range(BLOCKS):
                low(1, 0, kb)
            dve.wait_ge(x1_ready, BATCHES)
            with dve.Fori(1, GROUPS - 2) as g:
                f_group(g, 2)
            f_group(GROUPS - 2, 1)
            f_group(GROUPS - 1, 0)
            f_output(GROUPS - 1)

        @block.tensor
        def _(pe):
            def modulation(js):
                for j in js:
                    ins = pe.matmul(PB[:, j * BATCHES:(j + 1) * BATCHES], WMOD[:, j * EMB:(j + 1) * EMB],
                                    SILU[:, 0, :], start=True, stop=True)
                ins.then_inc(mod_ready, 1)

            pe.wait_ge(mod_loaded, 32)
            pe.wait_ge(silu_step, 3)
            modulation((0, 1))
            pe.wait_ge(eye_loaded, 16)

            def turn_x(b):
                wait(pe, xhat_ready, b.count(1, 1))
                if b.known in (0, 1, 2):
                    wait(pe, hT_ready, b.known)
                else:
                    wait(pe, x1_ready, b.count(1, -4))
                for t in range(TILES):
                    ins = pe.transpose(PA[:, t * LANES:(t + 1) * LANES], XH[:, t, :], EYE[:, :])
                ins.then_inc(xT_ready, 1)

            def project(b, which, w, ready, free, free_at):
                wait(pe, free, free_at)
                bank = projection_bank(b, which)
                for s in range(2):
                    ins = pe.matmul(bank[:, s * SEQ:(s + 1) * SEQ], w[:, s, :], HT[:, :], start=True, stop=True)
                ins.then_inc(ready, 1)

            def project_v(b):
                if b.known in (0, 1, 2):
                    wait(pe, v_copied, b.known)
                else:
                    wait(pe, turned_k, b.count(1, 1))
                bank = projection_bank(b, "v")
                for t in range(TILES):
                    ins = pe.matmul(bank[:, t * LANES:(t + 1) * LANES], HT[:, t * LANES:(t + 1) * LANES],
                                    WV[:, :], start=True, stop=True)
                ins.then_inc(v_ready, 1)

            def scores_for_max(b, h, at=None):
                at = h if at is None else at
                base, n = 64 * (h % 2), h // 2
                if h < 2:
                    wait(pe, stack_ready[h][b.slot], b.in_slot(16 * STACK_DMAS))
                wait(pe, max_ready, b.count(HEADS, s1_bank_read(at)))
                rows = ST[b.slot][base:base + STACK, n, :, :]
                for t in range(TILES):
                    ins = pe.matmul(S1[s1_bank(at)][:, t, :], rows[:, 0, t * LANES:(t + 1) * LANES], rows[:, 1, :],
                                    start=True, stop=True)
                ins.then_inc(s1_ready, 1)

            def turn_max(b):
                wait(pe, mparts_ready, b.count(1, 1))
                wait(pe, yT_copied, b.count(1, -1))
                if b.known == 0:
                    pe.wait_ge(grows_copied, 1)
                    pe.wait_ge(eyeb_set, 1)
                for t in range(TILES):
                    ins = pe.transpose(MT_PSUM[:, t * LANES:(t + 1) * LANES],
                                       NPART[:, t, :], EYEB[:, :])
                ins.then_inc(mT_ready, 1)

            def shifted_scores(b, h):
                base, n = 64 * (h % 2), h // 2
                if h < 2:
                    wait(pe, mrows_ready[h][b.slot], b.in_slot(16))
                wait(pe, exp_ready, b.count(HEADS, h - 1))
                rows = ST[b.slot][base:base + SCORE_ROWS, n, :, :]
                for t in range(TILES):
                    ins = pe.matmul(S2[h % 2][:, t, :], rows[:, 1, t * LANES:(t + 1) * LANES], rows[:, 0, :],
                                    start=True, stop=True)
                ins.then_inc(s2_ready, 1)

            def weigh_values(b, quad, t):
                if t == 0:
                    wait(pe, exp_ready, b.count(HEADS, QUAD * quad + QUAD))
                    wait(pe, v_copied, 3 if b.known == 0 else b.count(1, 1))
                    wait(pe, ot_copied, b.count(2, quad // 2))
                for c in range(QUAD):
                    h = QUAD * quad + c
                    ins = pe.matmul(OT[32 * c:32 * c + 32, quad % 2, :], VS[b.slot][:, t, h, :],
                                    PT[:, h % (2 * QUAD), t, :], start=(t == 0), stop=(t == TILES - 1))
                if t == TILES - 1:
                    ins.then_inc(pv_ready, 1)

            def turn_y(b, t):
                if t == 0:
                    wait(pe, ot_copied, b.count(2, 2))
                    wait(pe, mT_copied, b.capped(2))
                else:
                    wait(pe, y_normed, b.count(2, 1))
                for q in range(HEADS // QUAD):
                    ins = pe.transpose(PB[:, q * LANES:(q + 1) * LANES], OTS[:, q, t * LANES:(t + 1) * LANES], EYE[:, :])
                ins.then_inc(y_turned, 1)

            def turn_y_back(b):
                wait(pe, y_normed, b.count(2, 2))
                for t in range(TILES):
                    ins = pe.transpose(PB[:, t * LANES:(t + 1) * LANES], YN[:, t, :], EYE[:, :])
                ins.then_inc(yT_ready, 1)

            def project_out(b):
                wait(pe, yT_copied, b.count(1, 1))
                wait(pe, wog_ready, b.count(1, 1))
                wait(pe, v_copied, b.capped(5))
                for t in range(TILES):
                    ins = pe.matmul(PA[:, t * LANES:(t + 1) * LANES], YT[:, t * LANES:(t + 1) * LANES], WOG[:, :],
                                    start=True, stop=True)
                ins.then_inc(o_ready, 1)

            def iteration(b):
                tail, prep = b.plus(-1), b.plus(3)
                for h in range(HEADS):
                    if b.exists():
                        shifted_scores(b, h)
                    m = b.plus(1 + (h + LEAD) // HEADS)
                    if m.exists():
                        scores_for_max(m, (h + LEAD) % HEADS)
                    if tail.exists():
                        if h in (0, 1):
                            weigh_values(tail, 3, h)
                        if h == PE_AT["turn_y0"]:
                            turn_y(tail, 0)
                        if h == PE_AT["turn_y1"]:
                            turn_y(tail, 1)
                        if h == PE_AT["turn_y_back"]:
                            turn_y_back(tail)
                        if h == PE_AT["out"]:
                            project_out(tail)
                    if b.exists() and h in PE_AT["values"]:
                        step = PE_AT["values"].index(h)
                        weigh_values(b, step // TILES, step % TILES)
                    if prep.exists():
                        if h == PE_AT["turn_x"]:
                            turn_x(prep)
                        if h == PE_AT["q"]:
                            project(prep, "q", WQ, q_ready, hT_ready, prep.count(1, 1))
                        if h == PE_AT["k"]:
                            project(prep, "k", WK, k_ready, turned_q, prep.count(1, 1))
                        if h == PE_AT["v"]:
                            project_v(prep)
                    if b.plus(1).exists() and h == PE_AT["turn_max"]:
                        turn_max(b.plus(1))
                    if b.known == BATCHES - 1:
                        if h == FIRST_AT["turn"]:
                            pe.wait_ge(v_copied, BATCHES)
                            pe.wait_ge(x1_ready, BATCHES - 2)
                            f_turn(0)
                        if h == FIRST_AT["blocks"][0]:
                            pe.wait_ge(max_ready, HEADS * BATCHES)
                            pe.wait_ge(fw_ready, 3)
                            pe.wait_ge(f_hT, 1)
                        if h in FIRST_AT["blocks"]:
                            f_layer0(0, (FIRST_AT["blocks"].index(h),))

            def f_turn(g):
                pe.wait_ge(f_xhat, g + 1)
                if not isinstance(g, int) or g > 0:
                    pe.wait_ge(f_hT, g)
                for t in range(GROUP):
                    ins = pe.transpose(PA[:, t * LANES:(t + 1) * LANES], FXH[:, t, :], EYE[:, :])
                ins.then_inc(f_xT, 1)

            def f_layer0(g, blocks=range(BLOCKS)):
                if 0 in blocks:
                    pe.wait_ge(f_hhi, g + 1)
                    pe.wait_ge(f_hlo, g + 1)
                for f in blocks:
                    if isinstance(g, int) and g == 0:
                        if f == 3:
                            pe.wait_ge(lo_ready, 1)
                    elif f > 0:
                        pe.wait_ge(lo_ready, g * 8 + (f - 4))
                    w = W0[:, f * LANES:(f + 1) * LANES]
                    pe.matmul(layer_bank(g, 0, f), w, FHHI[:, :], start=True, stop=False)
                    pe.matmul(layer_bank(g, 0, f), w, FHLO[:, :], start=False, stop=True).then_inc(block_ready, 1)

            def f_layer1(g, f):
                if f == 0:
                    pe.wait_ge(lo_ready, g * 8 + (3 if isinstance(g, int) else 2))
                for kb in range(BLOCKS):
                    if f == 0:
                        pe.wait_ge(lo_ready, g * 8 + (kb + 1))
                    w = W1[:, kb, f * LANES:(f + 1) * LANES]
                    pe.matmul(layer_bank(g, 1, f), w, HI[0][:, kb, :], start=(kb == 0), stop=False)
                    ins = pe.matmul(layer_bank(g, 1, f), w, LO[0][:, kb, :], start=False, stop=(kb == BLOCKS - 1))
                ins.then_inc(block_ready, 1)

            def f_layer2(g):
                if not isinstance(g, int) or g > 0:
                    pe.wait_ge(y_gated, g)
                for kb in range(BLOCKS):
                    pe.wait_ge(lo_ready, g * 8 + (kb + 5))
                    pe.matmul(PB[:, :], W2[:, kb, :], HI[1][:, kb, :], start=(kb == 0), stop=False)
                    ins = pe.matmul(PB[:, :], W2[:, kb, :], LO[1][:, kb, :], start=False, stop=(kb == BLOCKS - 1))
                ins.then_inc(y_ready, 1)

            def f_turn_back(g):
                pe.wait_ge(y_gated, g + 1)
                if not isinstance(g, int) or g > 0:
                    pe.wait_ge(out_ready, g)
                for t in range(GROUP):
                    ins = pe.transpose(OT[:, t // 2, (t % 2) * LANES:(t % 2 + 1) * LANES],
                                       FY[:, t // 2, (t % 2) * LANES:(t % 2 + 1) * LANES], EYE[:, :])
                ins.then_inc(y_back, 1)

            def f_group(g, more):
                f_layer1(g, 0)
                if more:
                    f_turn(g + 1)
                f_turn_back(g - 1)
                f_layer1(g, 1)
                f_layer1(g, 2)
                f_layer1(g, 3)
                if more:
                    f_layer0(g + 1)
                f_layer2(g)


            def prepare(b, between=lambda n: None):
                turn_x(b)
                if b.known == 0:
                    pe.wait_ge(wqk_loaded, 32)
                if b.known == 1:
                    pe.wait_ge(gates_loaded, 32)
                    modulation((2, 3, 4, 5))
                between(0)
                wait(pe, turned_q, b.known)
                project(b, "q", WQ, q_ready, hT_ready, b.count(1, 1))
                between(1)
                project(b, "k", WK, k_ready, turned_k, b.known)
                between(2)
                if b.known == 0:
                    pe.wait_ge(wv_loaded, 16)
                project_v(b)

            def first_scores(n):
                for at in (range(0, 3), range(3, 5), range(5, 7), range(7, HEADS))[n]:
                    scores_for_max(Batch(0, 0), FIRST_ORDER[at], at)

            def turn_gates():
                pe.wait_ge(mod_step, 8)
                pe.transpose(PB[0:BATCHES, 0:EMB], MOD[:, 2, :], EYE[:, :]).then_inc(gates_turned, 1)

            prepare(Batch(0, 0))
            prepare(Batch(0, 1))
            turn_gates()
            prepare(Batch(0, 2), first_scores)
            first_scores(3)
            turn_max(Batch(0, 0))
            for h in range(LEAD):
                scores_for_max(Batch(0, 1), h)
            iteration(Batch(0, 0))
            with pe.Fori(0, 3) as turn:
                for j in range(RING):
                    iteration(Batch(turn, 1 + j))
            for b in range(13, BATCHES - 1):
                iteration(Batch(0, b))

            last = Batch(0, BATCHES - 1)
            iteration(last)
            weigh_values(last, 3, 0)
            weigh_values(last, 3, 1)
            pe.wait_ge(exp_ready, HEADS * BATCHES)
            pe.wait_ge(x1_ready, BATCHES - 1)
            f_turn(1)
            turn_y(last, 0)
            f_layer1(0, 0)
            turn_y(last, 1)
            f_layer1(0, 1)
            turn_y_back(last)
            f_layer1(0, 2)
            pe.wait_ge(f_hT, 2)
            project_out(last)
            f_layer1(0, 3)
            f_layer0(1)
            f_layer2(0)
            pe.wait_ge(x1_ready, BATCHES)
            with pe.Fori(1, GROUPS - 1) as g:
                f_group(g, True)
            f_group(GROUPS - 1, False)
            f_turn_back(GROUPS - 1)


def rope_table():
    i = np.arange(HEAD_DIM // 2, dtype=np.float32)
    rate = np.power(np.float32(10000.0), np.float32(2.0) * i / np.float32(HEAD_DIM))
    theta = np.arange(SEQ, dtype=np.float32)[:, None] * rate[None, :]
    theta = theta.astype(np.float64)
    cos, sin = np.cos(theta), np.sin(theta)
    position = np.arange(SEQ).reshape(LANES, TILES).T.reshape(-1)
    table = np.zeros((LANES, 2, 2, SEQ), np.float64)
    for p in range(LANES):
        d = p % 64 // (HEADS // 2)
        for s, scale in enumerate((1.0 / np.sqrt(HEAD_DIM), 1.0)):
            table[p, s, 0] = cos[position, d // 2] * scale
            table[p, s, 1] = sin[position, d // 2] * scale * (1 if d % 2 else -1)
    return table.reshape(LANES, 2, 2 * SEQ).astype(np.float32)


def kernel(**inputs):
    import concourse.bacc as _bacc
    from concourse.bass_utils import run_bass_kernel_spmd as _run

    a = {k: np.asarray(v) for k, v in inputs.items()}

    def plain_and_swapped(w):
        w = w.reshape(HEADS // 2, 2, HEAD_DIM // 2, 2, EMB)
        both = np.stack([w, w[:, :, :, ::-1]], 0).reshape(2, HEADS // 2, 2, HEAD_DIM, EMB)
        return both.transpose(4, 0, 2, 3, 1).reshape(EMB, 2, EMB)

    arrays = {
        "x": a["L0_attn_x"],
        "wq": plain_and_swapped(a["L0_attn_w_q"]),
        "wk": plain_and_swapped(a["L0_attn_w_k"]),
        "wv": a["L0_attn_w_v"].T,
        "wo": a["L0_attn_w_o"].T,
        "rope": rope_table(),
        "eye": np.eye(LANES, dtype=np.float32),
        "c_t": a["L0_c"].T,
        "wmod": a["L0_wmod"],
        "k0": a["L0_ffn_k0"],
        "k1": a["L0_ffn_k1"],
        "k2": a["L0_ffn_k2"],
        "scales": np.stack([a["L0_ffn_s0"], a["L0_ffn_s1"], a["L0_ffn_s2"]]).reshape(1, 3),
    }
    arrays = {k: np.ascontiguousarray(v) for k, v in arrays.items()}
    nc = _bacc.Bacc("TRN2", target_bir_lowering=False, num_devices=1)
    args = [nc.dram_tensor(f"in_{k}", v.shape, mybir.dt.from_np(v.dtype), kind="ExternalInput").ap()
            for k, v in arrays.items()]
    out = nc.dram_tensor("out", (BATCHES, SEQ, EMB), mybir.dt.float32, kind="ExternalOutput").ap()
    gate_rows = nc.dram_tensor("gate_rows", (BATCHES, EMB), mybir.dt.float32, kind="Internal").ap()
    adaln_block(nc, *args, gate_rows, out)
    r = _run(nc, [{f"in_{k}": v for k, v in arrays.items()}], core_ids=[0])
    return r.results[0]["out"]
```
